# Optimizing a Trainium2 kernel written in Bass

```python
import numpy as np
import jax
import jax.numpy as jnp

def _softmax(x, axis=-1):
    return jax.nn.softmax(x, axis=axis)

def _gelu(x):
    return jax.nn.gelu(x, approximate=True)

def _silu(x):
    return jax.nn.silu(x)

def _sigmoid(x):
    return jax.nn.sigmoid(x)

def _layernorm(x, axis=-1, eps=1e-05):
    m = jnp.mean(x, axis=axis, keepdims=True)
    v = jnp.var(x, axis=axis, keepdims=True)
    return (x - m) / jnp.sqrt(v + eps)

def _scatter_add(tgt, idx, src, axis=0):
    return tgt.at[idx].add(src)

def _segment_sum(src, seg, n):
    return jax.ops.segment_sum(src, seg, n)
kernel_name = 'mk_gnn_preln_d4_gnn_r8_1de7f8'

def setup_inputs(seed: int=0):
    np.random.seed(seed)
    _w = jnp.asarray

    def _rec_inputs():
        import jax
        import jax.numpy as jnp
        _gk = jax.random.key(seed)
        x = -7.329e-05 + 0.9999 * jax.random.normal(jax.random.fold_in(_gk, 1), (1250, 1024), jnp.float32)
        src = jax.random.randint(jax.random.fold_in(_gk, 2), (20000,), 0, 1250, jnp.int32)
        dst = jax.random.randint(jax.random.fold_in(_gk, 3), (20000,), 0, 1250, jnp.int32)
        _o = jnp.argsort(dst, stable=True)
        src = src[_o]
        dst = dst[_o]
        edge_type_8 = jax.random.randint(jax.random.fold_in(_gk, 13), (20000,), 0, 8, jnp.int32)
        edge_weight = -0.000130211 + 0.031236 * jax.random.normal(jax.random.fold_in(_gk, 14), (20000,), jnp.float32)
        return (x, src, dst, edge_type_8, edge_weight)
    x, src, dst, edge_type_8, edge_weight = _rec_inputs()

    def _L0_gnn_setup():
        import jax, jax.numpy as jnp
        import numpy as np
        INDIM = 1024
        OUTDIM = 1024
        NNZ = 8192
        N = 6250
        key = jax.random.key(seed)
        k1, k2, k3, k4, k5 = jax.random.split(key, 5)
        x = jax.random.normal(k1, (N, INDIM), dtype=jnp.float32)
        stdv = np.sqrt(6.0 / (INDIM + OUTDIM))
        nnz_weight = jax.random.uniform(k2, (NNZ,), dtype=jnp.float32, minval=-stdv, maxval=stdv)
        bias = jax.random.normal(k3, (OUTDIM,), dtype=jnp.float32) * 0.02
        row = jax.random.randint(k4, (NNZ,), 0, OUTDIM, dtype=jnp.int64)
        col = jax.random.randint(k5, (NNZ,), 0, INDIM, dtype=jnp.int64)
        edge_index = jnp.stack([row, col])
        return {'x': x, 'nnz_weight': nnz_weight, 'bias': bias, 'edge_index': edge_index}
    _L0_gnn_all = _L0_gnn_setup()
    _L0_gnn_in = {k: v for k, v in _L0_gnn_all.items() if k in ('bias',)}
    del _L0_gnn_all

    def _L1_gnn_setup():
        import jax, jax.numpy as jnp
        import numpy as np
        N_NODES = 3125
        N_EDGES = 50000
        D = 1024

        def _sage_layer(h, edge_src, edge_dst, deg_inv, W_self, W_neigh, b):
            msg = h[edge_src]
            agg = jax.ops.segment_sum(msg, edge_dst, num_segments=h.shape[0])
            mean = agg * deg_inv[:, None]
            return h @ W_self + mean @ W_neigh + b
        key = jax.random.key(seed)
        ks = jax.random.split(key, 8)
        s = 1.0 / np.sqrt(D)
        return {'x': jax.random.normal(ks[0], (N_NODES, D), dtype=jnp.float32), 'edge_src': jax.random.randint(ks[1], (N_EDGES,), 0, N_NODES, dtype=jnp.int32), 'edge_dst': jax.random.randint(ks[2], (N_EDGES,), 0, N_NODES, dtype=jnp.int32), 'W_self0': jax.random.normal(ks[3], (D, D), dtype=jnp.float32) * s, 'W_neigh0': jax.random.normal(ks[4], (D, D), dtype=jnp.float32) * s, 'b0': jnp.zeros((D,), dtype=jnp.float32), 'W_self1': jax.random.normal(ks[5], (D, D), dtype=jnp.float32) * s, 'W_neigh1': jax.random.normal(ks[6], (D, D), dtype=jnp.float32) * s, 'b1': jnp.zeros((D,), dtype=jnp.float32)}
    _L1_gnn_all = _L1_gnn_setup()
    _L1_gnn_in = {k: v for k, v in _L1_gnn_all.items() if k in ('W_self0', 'W_neigh0', 'b0', 'W_self1', 'W_neigh1', 'b1')}
    del _L1_gnn_all

    def _L2_gnn_setup():
        import jax, jax.numpy as jnp
        import numpy as np
        N_NODES = 1250
        N_EDGES = 20000
        DIM = 1024
        key = jax.random.key(seed)
        k1, k2, k3 = jax.random.split(key, 3)
        x = jax.random.normal(k1, (N_NODES, DIM), dtype=jnp.float32)
        edge_index = jax.random.randint(k2, (2, N_EDGES), 0, N_NODES, dtype=jnp.int64)
        W = jax.random.normal(k3, (DIM, DIM), dtype=jnp.float32) * (1.0 / np.sqrt(DIM))
        b = jnp.zeros((DIM,), dtype=jnp.float32)
        return {'x': x, 'edge_index': edge_index, 'W': W, 'b': b}
    _L2_gnn_all = _L2_gnn_setup()
    _L2_gnn_in = {k: v for k, v in _L2_gnn_all.items() if k in ('W', 'b')}
    del _L2_gnn_all

    def _L3_gnn_setup():
        import jax, jax.numpy as jnp
        import numpy as np
        N, D, R, E = (1250, 1024, 8, 10000)

        def _rgcn(x, edge_index, edge_type, weight, root, bias):
            src, dst = (edge_index[0], edge_index[1])
            msgs = x[src]
            out = x @ root + bias
            n = x.shape[0]
            for r in range(weight.shape[0]):
                mask = (edge_type == r).astype(x.dtype)
                sums = jax.ops.segment_sum(msgs * mask[:, None], dst, num_segments=n)
                cnt = jax.ops.segment_sum(mask, dst, num_segments=n)
                mean = sums / jnp.maximum(cnt, 1.0)[:, None]
                out = out + mean @ weight[r]
            return out
        key = jax.random.key(seed)
        ks = jax.random.split(key, 8)
        s = 1.0 / np.sqrt(D)
        x = jax.random.normal(ks[0], (N, D), dtype=jnp.float32)
        edge_index = jax.random.randint(ks[1], (2, E), 0, N, dtype=jnp.int64)
        edge_type = jax.random.randint(ks[2], (E,), 0, R, dtype=jnp.int64)
        weight = jax.random.normal(ks[3], (R, D, D), dtype=jnp.float32) * s
        root = jax.random.normal(ks[4], (D, D), dtype=jnp.float32) * s
        bias = jnp.zeros((D,), dtype=jnp.float32)
        w_gate = jax.random.normal(ks[5], (2 * D, D), dtype=jnp.float32) * (1.0 / np.sqrt(2 * D))
        b_gate = jnp.zeros((D,), dtype=jnp.float32)
        return {'x': x, 'edge_index': edge_index, 'edge_type': edge_type, 'weight': weight, 'root': root, 'bias': bias, 'w_gate': w_gate, 'b_gate': b_gate}
    _L3_gnn_all = _L3_gnn_setup()
    _L3_gnn_in = {k: v for k, v in _L3_gnn_all.items() if k in ('weight', 'root', 'bias', 'w_gate', 'b_gate')}
    del _L3_gnn_all
    return {'x': x, 'src': src, 'dst': dst, 'edge_type_8': edge_type_8, 'edge_weight': edge_weight, 'L0_gnn_bias': _L0_gnn_in['bias'], 'L1_gnn_W_self0': _L1_gnn_in['W_self0'], 'L1_gnn_W_neigh0': _L1_gnn_in['W_neigh0'], 'L1_gnn_b0': _L1_gnn_in['b0'], 'L1_gnn_W_self1': _L1_gnn_in['W_self1'], 'L1_gnn_W_neigh1': _L1_gnn_in['W_neigh1'], 'L1_gnn_b1': _L1_gnn_in['b1'], 'L2_gnn_W': _L2_gnn_in['W'], 'L2_gnn_b': _L2_gnn_in['b'], 'L3_gnn_weight': _L3_gnn_in['weight'], 'L3_gnn_root': _L3_gnn_in['root'], 'L3_gnn_bias': _L3_gnn_in['bias'], 'L3_gnn_w_gate': _L3_gnn_in['w_gate'], 'L3_gnn_b_gate': _L3_gnn_in['b_gate']}

def reference(x, src, dst, edge_type_8, edge_weight, L0_gnn_bias, L1_gnn_W_self0, L1_gnn_W_neigh0, L1_gnn_b0, L1_gnn_W_self1, L1_gnn_W_neigh1, L1_gnn_b1, L2_gnn_W, L2_gnn_b, L3_gnn_weight, L3_gnn_root, L3_gnn_bias, L3_gnn_w_gate, L3_gnn_b_gate):
    import jax
    import jax.numpy as jnp

    def _L0_gnn_ref(x, nnz_weight, bias, edge_index):
        import jax, jax.numpy as jnp
        import numpy as np
        INDIM = 1024
        OUTDIM = 1024
        NNZ = 8192
        N = 6250
        row, col = (edge_index[0], edge_index[1])
        W = jnp.zeros((OUTDIM, INDIM), dtype=nnz_weight.dtype).at[row, col].add(nnz_weight)
        return x @ W.T + bias

    def _L1_gnn_ref(x, edge_src, edge_dst, W_self0, W_neigh0, b0, W_self1, W_neigh1, b1):
        import jax, jax.numpy as jnp
        import numpy as np
        N_NODES = 3125
        N_EDGES = 50000
        D = 1024

        def _sage_layer(h, edge_src, edge_dst, deg_inv, W_self, W_neigh, b):
            msg = h[edge_src]
            agg = jax.ops.segment_sum(msg, edge_dst, num_segments=h.shape[0])
            mean = agg * deg_inv[:, None]
            return h @ W_self + mean @ W_neigh + b
        N = x.shape[0]
        deg = jax.ops.segment_sum(jnp.ones_like(edge_dst, dtype=x.dtype), edge_dst, num_segments=N)
        deg_inv = 1.0 / jnp.maximum(deg, 1.0)
        h = jax.nn.relu(_sage_layer(x, edge_src, edge_dst, deg_inv, W_self0, W_neigh0, b0))
        out = _sage_layer(h, edge_src, edge_dst, deg_inv, W_self1, W_neigh1, b1)
        return out

    def _L2_gnn_ref(x, edge_index, W, b):
        import jax, jax.numpy as jnp
        import numpy as np
        N_NODES = 1250
        N_EDGES = 20000
        DIM = 1024
        'GCNConv (add_self_loops=True, symmetric norm) -> Dropout(eval=identity) -> ReLU.'
        n = x.shape[0]
        loops = jnp.arange(n, dtype=edge_index.dtype)
        src = jnp.concatenate([edge_index[0], loops])
        dst = jnp.concatenate([edge_index[1], loops])
        deg = jax.ops.segment_sum(jnp.ones_like(dst, dtype=x.dtype), dst, num_segments=n)
        dinv = jnp.where(deg > 0, jax.lax.rsqrt(deg), jnp.zeros_like(deg))
        norm = dinv[src] * dinv[dst]
        h = x @ W
        msg = h[src] * norm[:, None]
        out = jax.ops.segment_sum(msg, dst, num_segments=n) + b
        return jax.nn.relu(out)

    def _L3_gnn_ref(x, edge_index, edge_type, weight, root, bias, w_gate, b_gate):
        import jax, jax.numpy as jnp
        import numpy as np
        N, D, R, E = (1250, 1024, 8, 10000)

        def _rgcn(x, edge_index, edge_type, weight, root, bias):
            src, dst = (edge_index[0], edge_index[1])
            msgs = x[src]
            out = x @ root + bias
            n = x.shape[0]
            for r in range(weight.shape[0]):
                mask = (edge_type == r).astype(x.dtype)
                sums = jax.ops.segment_sum(msgs * mask[:, None], dst, num_segments=n)
                cnt = jax.ops.segment_sum(mask, dst, num_segments=n)
                mean = sums / jnp.maximum(cnt, 1.0)[:, None]
                out = out + mean @ weight[r]
            return out
        u = _rgcn(x, edge_index, edge_type, weight, root, bias)
        z = jnp.concatenate([u, x], axis=1) @ w_gate + b_gate
        h = jnp.tanh(u) * z + x * (1.0 - z)
        return h
    edge_index = jnp.stack([src, dst])
    h = jnp.maximum(_layernorm(x, axis=-1), 0.0)
    x = x + _L0_gnn_ref(h, edge_weight, L0_gnn_bias, edge_index)
    h = jnp.maximum(_layernorm(x, axis=-1), 0.0)
    x = x + _L1_gnn_ref(h, src, dst, L1_gnn_W_self0, L1_gnn_W_neigh0, L1_gnn_b0, L1_gnn_W_self1, L1_gnn_W_neigh1, L1_gnn_b1)
    h = jnp.maximum(_layernorm(x, axis=-1), 0.0)
    x = x + _L2_gnn_ref(h, edge_index, L2_gnn_W, L2_gnn_b)
    h = jnp.maximum(_layernorm(x, axis=-1), 0.0)
    x = x + _L3_gnn_ref(h, edge_index, edge_type_8, L3_gnn_weight, L3_gnn_root, L3_gnn_bias, L3_gnn_w_gate, L3_gnn_b_gate)
    return x

_drawn_inputs = setup_inputs


def setup_inputs(seed=0):
    import zlib

    import numpy as np

    out = dict(_drawn_inputs(seed))
    spreads = {'L1_gnn_b0': (0.0, 0.1),
     'L1_gnn_b1': (0.0, 0.1),
     'L2_gnn_b': (0.0, 0.1),
     'L3_gnn_bias': (0.0, 0.1),
     'L3_gnn_b_gate': (0.0, 0.1)}
    factors = {}
    for name, (base, spread) in spreads.items():
        noise = np.random.default_rng([zlib.crc32(name.encode()), seed]).standard_normal(out[name].shape)
        drawn = base * np.exp(spread * noise) if base else spread * noise
        out[name] = jnp.asarray(drawn.astype(out[name].dtype))
    for name, factor in factors.items():
        out[name] = (out[name] * factor).astype(out[name].dtype)
    return out
```

```python
import concourse.bass as bass
from concourse import mybir
from contextlib import ExitStack

FP32 = mybir.dt.float32
F32R = mybir.dt.float32r
I32 = mybir.dt.int32
ALU = mybir.AluOpType
ACT = mybir.ActivationFunctionType

P = 128
NODES = 1250
FEATURES = 1024
EDGES = 20000
RELATIONS = 8
HALF = FEATURES // 2
KT = HALF // P
TILES = -(-NODES // P)
ROWS = [min(P, NODES - P * n) for n in range(TILES)]
PADDED = TILES * P
CHUNKS = [(0, 4), (4, 7), (7, 10)]
WIDTH = [sum(ROWS[a:b]) for a, b in CHUNKS]
START = [P * a for a, _ in CHUNKS]
GROUPS = 2 * TILES
FRONTS = KT * len(CHUNKS)
EDGE_ROWS = 125
EDGE_COLS = EDGES // EDGE_ROWS
QUADS = EDGE_COLS // 4
TABLES = 4
NW = FEATURES * FEATURES
NA = PADDED * NODES
EPS = 1e-5

SOURCES = [("x", 0, True, True), ("x", 1, False, True),
           ("x1", 0, True, True), ("x1", 1, False, True), ("x1", 0, False, True),
           ("g", 0, True, False), ("g", 1, False, False),
           ("x2", 0, True, True), ("x2", 1, False, True),
           ("x3", 0, True, True), ("x3", 1, False, True),
           ("u", 0, True, False), ("u", 1, False, False),
           ("x3", 0, False, True), ("x3", 1, False, True)]
STEPS = [(False, 0, "edge", 0), (False, 1, "edge", 1),
         (False, 2, "self0", 0), (False, 3, "self0", 1), (True, 3, "neigh0", 1), (True, 4, "neigh0", 0),
         (False, 5, "self1", 0), (True, 5, "neigh1", 0), (False, 6, "self1", 1), (True, 6, "neigh1", 1),
         (True, 7, "gcn", 0), (True, 8, "gcn", 1),
         (False, 9, "root", 0)] + [(True, 9, "rel", 0)] * RELATIONS + [
         (False, 10, "root", 1)] + [(True, 10, "rel", 1)] * RELATIONS + [
         (False, 11, "gate", 0), (False, 12, "gate", 1), (False, 13, "gate", 2), (False, 14, "gate", 3)]
G_BEFORE = [sum(t[0] for t in STEPS[:s]) for s in range(len(STEPS))]
LAST = len(STEPS) - 1
EPOCHS = [(1, "add", "x1", "x", "b0", True), (5, "relu", "g", None, "b10", False),
          (9, "add", "x2", "x1", "b11", True), (11, "relu_add", "x3", "x2", "b2", True),
          (29, "none", "u", None, "b3", False), (LAST, "gate", "out", "x3", "bg", False)]
EPOCH_END = {e[0]: n for n, e in enumerate(EPOCHS)}
LAST_USE = [max(s for s, t in enumerate(STEPS) if t[1] == v) for v in range(len(SOURCES))]
FIRST_USE = [min(s for s, t in enumerate(STEPS) if t[1] == v) for v in range(len(SOURCES))]
SUM_AFTER = 3
MOMENTS = {-1: 0, 0: 1, 2: 2, 3: 3}
TAILS = {0: 0, 1: 1, 2: 2, 3: 3}

ROW_USES = []
for _v, (_, _, _from_acc, _) in enumerate(SOURCES):
    for _e, _ep in enumerate(EPOCHS[:-1]):
        if FIRST_USE[_v] == _ep[0] + 1 and _ep[3]:
            ROW_USES += [("rest", _e, n) for n in range(TILES)]
    if not _from_acc:
        ROW_USES += [("source", _v, n) for n in range(TILES)]
ROW_USES += [("rest", len(EPOCHS) - 1, n) for n in range(TILES)]
ROW_AT = {u: i for i, u in enumerate(ROW_USES)}


def build(nc, x, src, dst, etype, eweight, b0, self0, neigh0, b10, self1, neigh1, b11, gcn, b2, rel,
          root, b3, gate, bg, out):
    def dram(name, shape):
        return nc.dram_tensor(name, shape, FP32, kind="Internal").ap()

    wtab = [dram(f"wtab{j}", (NW + P, 1)) for j in range(TABLES)]
    atab = [dram(f"atab{j}", (NA + P, 1)) for j in range(TABLES)]
    rtab = dram("rtab", (RELATIONS * NA + P, 1))
    asum = dram("asum", (PADDED, NODES))
    aself = dram("aself", (PADDED, NODES))
    rows_of = {"x": x, "out": out}
    for name in ("x1", "x2", "x3", "g", "u"):
        rows_of[name] = dram(name, (NODES, FEATURES))
    weights = {"self0": self0, "neigh0": neigh0, "self1": self1, "neigh1": neigh1, "gcn": gcn,
               "root": root, "gate": gate, "rel": rel.rearrange("r k o -> (r k) o")}
    bias = {"b0": b0, "b10": b10, "b11": b11, "b2": b2, "b3": b3, "bg": bg}
    wtab2 = [t[0:NW].rearrange("(d s) c -> d (s c)", s=FEATURES) for t in wtab]
    atab2 = [t[0:NA].rearrange("(s d) c -> s (d c)", d=NODES) for t in atab]
    rtab2 = rtab[0:RELATIONS * NA].rearrange("(s d) c -> s (d c)", d=NODES)

    ctx = ExitStack()
    with ctx:
        base = nc.sbuf_base
        arena = ctx.enter_context(nc.sbuf_tensor("arena", [P, 212768], mybir.dt.uint8))
        top = [-(-base // 32) * 32]

        def place(name, shape, dt, at=None):
            size = 4
            for d in shape[1:]:
                size *= d
            if at is None:
                at = top[0]
                top[0] = -(-(at + size) // 32) * 32
                assert top[0] <= base + 212768, (name, top[0] - base)
            return nc.alloc_sbuf_tensor_at(name, shape, dt, offset=at)

        def sem(name):
            return ctx.enter_context(nc.semaphore(name))

        h_hi = place("h_hi", [P, TILES, HALF], F32R)
        h_lo = place("h_lo", [P, TILES, HALF], F32R)
        pt_hi = [place(f"pt_hi{i}", [P, KT, WIDTH[i]], F32R) for i in range(2)]
        pt_lo = [place(f"pt_lo{i}", [P, KT, WIDTH[i]], F32R) for i in range(2)]
        w_raw = place("w_raw", [P, KT, FEATURES], FP32)
        w_hi = place("w_hi", [P, KT, FEATURES], F32R)
        w_lo = place("w_lo", [P, KT, FEATURES], F32R)
        acc = place("acc", [P, TILES, FEATURES], FP32)
        counts_at = top[0]
        a_chunk = [place(f"a_chunk{i}", [P, TILES, WIDTH[i]], F32R) for i in range(2)]
        rows = place("rows", [P, 2, FEATURES], FP32)
        t_buf = place("t_buf", [P, 2, HALF], FP32)
        ident = place("ident", [P, P], F32R)
        ones2 = place("ones2", [P, 2], F32R)
        idx_r = place("idx_r", [P, EDGE_COLS], I32)
        cnt_r = place("cnt_r", [P, EDGE_COLS], FP32)
        idx_slot = place("idx_slot", [P, 2, 4], I32)
        val_slot = place("val_slot", [P, 2, 4], FP32)
        moments = place("moments", [P, TILES, 2], FP32)
        partial = place("partial", [P, 2, 2, 6], FP32)
        std = place("std", [P, TILES], FP32)
        scale = place("scale", [P, TILES], FP32)
        shift = place("shift", [P, TILES], FP32)
        deg_inv = place("deg_inv", [P, TILES], FP32)
        deg_std = place("deg_std", [P, TILES], FP32)
        dinv = place("dinv", [P, TILES], FP32)
        rel_inv = place("rel_inv", [P, RELATIONS * TILES], FP32)
        eps = place("eps", [P, 1], FP32)
        in_buf = place("in_buf", [P, 5, NODES], FP32, counts_at)
        sum_at = counts_at + -(-5 * NODES * 4 // 32) * 32
        sum_buf = place("sum_buf", [P, 2, NODES], F32R, sum_at)
        at = [counts_at]

        def prep(name, shape, dt):
            size = 4
            for d in shape[1:]:
                size *= d
            t = place(name, shape, dt, at[0])
            at[0] += -(-size // 32) * 32
            return t

        diag = prep("diag", [P, 2, 4, P], FP32)
        same = prep("same", [P, 2, 4, P], FP32)
        before = prep("before", [P, 2, 4, P], FP32)
        ident_f = prep("ident_f", [P, P], FP32)
        ones_f = prep("ones_f", [P, P], FP32)
        below = prep("below", [P, P], FP32)
        idx_w = prep("idx_w", [P, EDGE_COLS], I32)
        wsum = prep("wsum", [P, EDGE_COLS], FP32)
        key = [prep(f"key{i}", [P, EDGE_COLS], FP32) for i in range(2)]
        off = {name: prep(f"off_{name}", [P, EDGE_COLS], FP32) for name in "war"}
        one_w = prep("one_w", [P, 2 * EDGE_COLS], FP32)
        trash_i = prep("trash_i", [P, 1], I32)
        trash = {name: prep(f"trash_{name}", [P, 1], FP32) for name in "war"}
        idx_f = prep("idx_f", [P, 2, 2, 4], FP32)
        assert at[0] <= sum_at
        at[0] = sum_at
        idx_a = prep("idx_a", [P, EDGE_COLS], I32)
        cnt_a = prep("cnt_a", [P, EDGE_COLS], FP32)
        zeros = prep("zeros", [P, NODES], FP32)
        assert at[0] <= sum_at + 2 * NODES * 4
        at[0] = -(-(base) // 32) * 32
        edges_i = prep("edges_i", [P, 3, EDGE_COLS], I32)
        edges_f = prep("edges_f", [P, 3, EDGE_COLS], FP32)
        edge_w = prep("edge_w", [P, EDGE_COLS], FP32)
        valid = prep("valid", [P, 2, EDGE_COLS], FP32)
        src_row = prep("src_row", [P, EDGE_COLS], FP32)
        key_w = prep("key_w", [P, EDGE_COLS], FP32)

        banks = [ctx.enter_context(nc.psum_tensor(f"bank{i}", [P, 512], FP32)) for i in range(8)]
        front_bank, dense_bank, deg_bank = banks[0:3], banks[3:7], banks[7]
        cast_bank, stat_bank = banks[3:5], banks[5:7]

        edges_in = sem("edges_in")
        x_in = sem("x_in")
        consts = sem("consts")
        small = sem("small")
        keys_ready = sem("keys_ready")
        equal_done = sem("equal_done")
        row_done = sem("row_done")
        zeroed = {name: sem(f"zeroed_{name}") for name in "war"}
        diag_ready = sem("diag_ready")
        cast_done = sem("cast_done")
        same_ready = sem("same_ready")
        stat_done = sem("stat_done")
        idx_ready = sem("idx_ready")
        slot_ready = sem("slot_ready")
        added = {"w": [sem(f"added_w{j}") for j in range(TABLES)],
                 "a": [sem(f"added_a{j}") for j in range(TABLES)], "r": [sem("added_r")]}
        in_loaded = [sem(f"in_loaded{i}") for i in range(5)]
        t0_loaded = [sem(f"t0_loaded{i}") for i in range(2)]
        in_added = sem("in_added")
        counts_stored = [sem(f"counts_stored{i}") for i in range(2)]
        self_added = sem("self_added")
        self_stored = [sem(f"self_stored{i}") for i in range(2)]
        raw_loaded = [sem(f"raw_loaded{k}") for k in range(KT)]
        w_hi_ready = sem("w_hi_ready")
        w_lo_ready = sem("w_lo_ready")
        a_loaded = [sem(f"a_loaded{i}") for i in range(2)]
        front_done = sem("front_done")
        front_hi = sem("front_hi")
        front_lo = sem("front_lo")
        dense_done = sem("dense_done")
        acc_done = sem("acc_done")
        deg_done = sem("deg_done")
        deg_used = sem("deg_used")
        deg_piece = sem("deg_piece")
        deg_root = sem("deg_root")
        deg_small = sem("deg_small")
        moments_ready = sem("moments_ready")
        std_ready = sem("std_ready")
        norm_ready = sem("norm_ready")
        tail_done = sem("tail_done")
        rows_loaded = [sem(f"rows_loaded{i}") for i in range(2)]
        u_loaded = [sem(f"u_loaded{i}") for i in range(2)]
        t_ready = sem("t_ready")
        h_hi_ready = sem("h_hi_ready")
        h_ready = sem("h_ready")
        stored = [sem(f"stored{i}") for i in range(2)]
        acc_set = sem("acc_set")
        gate_act = sem("gate_act")
        out_ready = sem("out_ready")

        block = ctx.enter_context(nc.Block())

        def row_free(use):
            kind, which, n = ROW_USES[use]
            if kind == "source":
                return t_ready, TILES * which + n + 1
            if which == len(EPOCHS) - 1:
                return out_ready, n + 1
            return tail_done, TILES * TAILS[which] + n + 1

        @block.sync
        def _(sp):
            sp.wait_ge(consts, 1)
            for i, a in enumerate((src, dst, etype)):
                sp.dma_start(edges_i[0:EDGE_ROWS, i, :], a.rearrange("(p t) -> p t", p=EDGE_ROWS)).then_inc(edges_in, 16)
            sp.dma_start(edge_w[0:EDGE_ROWS, :], eweight.rearrange("(p t) -> p t", p=EDGE_ROWS)).then_inc(edges_in, 16)
            sp.wait_ge(consts, 2)
            for name, tabs, n in (("w", wtab, NW), ("x", None, 0), ("a", atab, NA), ("r", [rtab], NA)):
                if name == "x":
                    full = TILES - 1
                    sp.dma_start(acc[:, 0:full, :], x[0:full * P, :].rearrange("(n p) f -> p n f", p=P)).then_inc(x_in, 16)
                    sp.dma_start(acc[0:ROWS[full], full, :], x[full * P:, :]).then_inc(x_in, 16)
                    continue
                width = FEATURES if name == "w" else NODES
                for tab in tabs:
                    for r in range(RELATIONS if name == "r" else 1):
                        piece = tab[r * n:(r + 1) * n].rearrange("(p c w) o -> p c (w o)", p=P, w=width)
                        sp.dma_start(piece, zeros[:, None, 0:width].to_broadcast((P, piece.shape[1], width))).then_inc(zeroed[name], 16)

            def load_weights(s, first_row, name):
                for k in range(KT):
                    if k == 0 and not (isinstance(s, int) and s == 0):
                        sp.wait_ge(w_lo_ready, KT * s)
                    sp.dma_start(w_raw[:, k, :], weights[name][bass.ds(first_row + P * k, P), :]).then_inc(raw_loaded[k], 16)

            def load_in(q, src_ap):
                if q >= 5:
                    sp.wait_ge(in_added, q - 4)
                sp.dma_start(in_buf[:, q % 5, 0:src_ap.shape[1]], src_ap).then_inc(in_loaded[q % 5], 16)

            def load_edge_weights(s):
                if s == 0:
                    sp.wait_ge(idx_ready, 1 + 2 * QUADS)
                    for j in range(TABLES):
                        sp.wait_ge(added["w"][j], 16 * (1 + QUADS))
                for k in range(KT):
                    d = HALF * s + P * k
                    if s and k == 0:
                        sp.wait_ge(w_lo_ready, KT * s)
                    sp.dma_start(w_raw[:, k, :], wtab2[0][d:d + P, :]).then_inc(raw_loaded[k], 16)
                    for j in range(1, TABLES):
                        load_in(12 * s + 3 * k + j - 1, wtab2[j][d:d + P, :])

            def sum_counts():
                for j in range(TABLES):
                    sp.wait_ge(added["a"][j], 16 * (1 + QUADS))
                sp.wait_ge(zeroed["r"], 16 * RELATIONS)
                for n in range(TILES):
                    r = slice(P * n, P * n + P)
                    if n >= 2:
                        sp.wait_ge(self_stored[n % 2], 16 * (n // 2))
                    sp.dma_start(sum_buf[:, n % 2, :].bitcast(FP32), atab2[0][r, :]).then_inc(t0_loaded[n % 2], 16)
                    for j in range(1, TABLES):
                        load_in(24 + 3 * n + j - 1, atab2[j][r, :])

            def table_of(s):
                return {"neigh0": asum, "neigh1": asum, "gcn": aself}.get(STEPS[s][2])

            def load_counts(c, g, tab, first_row, fronts_then=None):
                cols = slice(START[c], START[c] + WIDTH[c])
                region = a_chunk[c % 2][:, :, 0:WIDTH[c]].bitcast(FP32)
                if tab is rtab2:
                    sp.wait_ge(added["r"][0], 16 * (1 + EDGE_COLS))
                if fronts_then is not None:
                    sp.wait_ge(front_done, fronts_then)
                sp.dma_start(region, tab[bass.ds(first_row, PADDED), cols].rearrange("(n p) d -> p n d", p=P)).then_inc(a_loaded[c % 2], 16)

            def load_row(u, ap, width):
                if u >= 2:
                    sp.wait_ge(*row_free(u - 2))
                sp.dma_start(rows[0:ap.shape[0], u % 2, 0:width], ap).then_inc(rows_loaded[u % 2], 16)

            def source(v):
                name, half, _, _ = SOURCES[v]
                for n in range(TILES):
                    load_row(ROW_AT["source", v, n], rows_of[name][P * n:P * n + ROWS[n], HALF * half:HALF * (half + 1)], HALF)

            def epoch_end(e):
                last, how, to, rest, _, _ = EPOCHS[e]
                v = next(v for v in range(len(SOURCES)) if FIRST_USE[v] == last + 1)
                for j in range(TILES + 2):
                    if rest and j < TILES:
                        load_row(ROW_AT["rest", e, j], rows_of[rest][P * j:P * j + ROWS[j], :], FEATURES)
                    n = j - 1
                    if 0 <= n < TILES:
                        if how == "none":
                            sp.wait_ge(acc_done, GROUPS * last + 2 * (n + 1))
                        else:
                            sp.wait_ge(tail_done, TILES * TAILS[e] + n + 1)
                        sp.dma_start(rows_of[to][P * n:P * n + ROWS[n], :], acc[0:ROWS[n], n, :]).then_inc(stored[n % 2], 16)
                    n = j - 2
                    if 0 <= n:
                        sp.wait_ge(stored[n % 2], 16 * (5 * e + n // 2 + 1))
                        set_acc(e + 1, v, n)

            def set_acc(e, v, n):
                sp.wait_ge(t_ready, TILES * v + n + 1)
                b = bias[EPOCHS[e][4]].rearrange("(o f) -> o f", o=1)
                sp.dma_start(acc[0:ROWS[n], n, :], b.to_broadcast((ROWS[n], FEATURES))).then_inc(acc_set, 16)

            for n in range(TILES):
                set_acc(0, 0, n)
            s = 0
            while s < len(STEPS):
                graph, v, name, half = STEPS[s]
                g = G_BEFORE[s]
                if name == "rel":
                    with sp.Fori(0, RELATIONS) as r:
                        fronts_then = [sp.snap(FRONTS * (s + r) + o) for o in (2 * KT - FRONTS, 0, KT)]
                        first = sp.snap(r * PADDED)
                        load_weights(s + r, r * FEATURES + HALF * half, "rel")
                        for c, then in ((1, 0), (0, 1), (2, 2)):
                            load_counts(c, g + r, rtab2, first, fronts_then[then])
                    s += RELATIONS
                else:
                    if name != "edge":
                        load_weights(s, HALF * half, name)
                    if graph:
                        sp.wait_ge(front_done, FRONTS * s - FRONTS + 2 * KT)
                        load_counts(1, g, table_of(s), 0)
                        sp.wait_ge(front_done, FRONTS * s)
                        load_counts(0, g, table_of(s), 0)
                    if FIRST_USE[v] == s:
                        if s - 1 in EPOCH_END:
                            epoch_end(EPOCH_END[s - 1])
                        if not SOURCES[v][2]:
                            source(v)
                    if name == "edge":
                        load_edge_weights(s)
                    if graph:
                        sp.wait_ge(front_done, FRONTS * s + KT)
                        load_counts(2, g, table_of(s), 0)
                    if s == SUM_AFTER:
                        sum_counts()
                        for i in range(2):
                            sp.wait_ge(counts_stored[i], 16 * (TILES // 2))
                            sp.wait_ge(self_stored[i], 16 * (TILES // 2))
                    s += 1
            e = len(EPOCHS) - 1
            for j in range(TILES + 1):
                if j < TILES:
                    load_row(ROW_AT["rest", e, j], rows_of["x3"][P * j:P * j + ROWS[j], :], FEATURES)
                    if j >= 2:
                        sp.wait_ge(out_ready, j - 1)
                    else:
                        sp.wait_ge(w_lo_ready, KT * len(STEPS))
                    sp.dma_start(w_raw[0:ROWS[j], j % 2, :], rows_of["u"][P * j:P * j + ROWS[j], :]).then_inc(u_loaded[j % 2], 16)
                n = j - 1
                if n >= 0:
                    sp.wait_ge(out_ready, n + 1)
                    sp.dma_start(out[P * n:P * n + ROWS[n], :], acc[0:ROWS[n], n, :]).then_inc(stored[n % 2], 16)
            for i in range(2):
                sp.wait_ge(stored[i], 16 * 5 * len(EPOCHS))

        @block.gpsimd
        def _(pool):
            pool.memset(edges_i[:, :, :], 2000)
            pool.memset(edge_w[:, :], 0.0).then_inc(consts, 1)
            pool.memset(zeros[:, :], 0.0).then_inc(consts, 1)
            pool.memset(ones_f[:, :], 1.0).then_inc(consts, 1)
            pool.memset(eps[:, :], EPS).then_inc(consts, 1)
            pool.iota(trash_i[:, :], pattern=[[0, 1]], base=0, channel_multiplier=1).then_inc(consts, 1)
            pool.wait_ge(consts, 5)
            pool.affine_select(out=ident_f[:, :], in_=ones_f[:, :], compare_op=ALU.is_equal, fill=0.0, base=0,
                               pattern=[[-1, P]], channel_multiplier=1).then_inc(consts, 1)
            pool.affine_select(out=below[:, :], in_=ones_f[:, :], compare_op=ALU.is_gt, fill=0.0, base=0,
                               pattern=[[1, P]], channel_multiplier=-1).then_inc(consts, 1)

            for name, tabs in (("w", wtab), ("a", atab), ("r", [rtab])):
                for tab, link in zip(tabs, added[name]):
                    pool.dma_start(tab[tab.shape[0] - P:], zeros[:, 0:1]).then_inc(link, 16)

            copied = 0
            for name, idx, val, tabs, ready in (("w", idx_w, wsum, wtab, 0), ("a", idx_a, cnt_a, atab, 0),
                                                ("r", idx_r, cnt_r, [rtab], QUADS)):
                sems, T = added[name], len(tabs)
                zeros_of = 16 * (TABLES if T > 1 else RELATIONS)
                per = 4 // T
                with pool.Fori(0, QUADS // 2) as i:
                    for b in range(2):
                        q = 2 * i + b
                        over = [pool.snap(pool.to_reg(16 * (1 + per * q + j))) for j in range(per)]
                        copies = pool.snap(pool.to_reg(q + 1 + copied))
                        pool.wait_ge(idx_ready, 1 + q + 1 + ready)
                        pool.tensor_copy(idx_slot[:, b, :], idx[:, bass.ds(4 * q, 4)])
                        pool.tensor_copy(val_slot[:, b, :], val[:, bass.ds(4 * q, 4)]).then_inc(slot_ready, 1)
                        pool.wait_ge(zeroed[name], zeros_of)
                        pool.wait_ge(slot_ready, copies)
                        for j in range(4):
                            if j:
                                pool.wait_ge(zeroed[name], zeros_of)
                            pool.wait_ge(sems[j % T], over[j // T])
                            pool.indirect_dma_start(
                                out=tabs[j % T], out_offset=bass.IndirectOffsetOnAxis(ap=idx_slot[:, b, j:j + 1], axis=0),
                                in_=val_slot[:, b, j:j + 1], in_offset=None, compute_op=ALU.add).then_inc(sems[j % T], 16)
                for j in range(T):
                    pool.wait_ge(sems[j], 16 * (1 + per * QUADS))
                copied += QUADS

        @block.scalar
        def _(act):
            def store_self(eng, n):
                eng.wait_ge(self_added, n + 1)
                eng.dma_start(aself[P * n:P * n + P, :], sum_buf[:, n % 2, :].bitcast(FP32)).then_inc(self_stored[n % 2], 16)

            def pt_slot_free(s, c):
                value = GROUPS * s + (0, -GROUPS + 2 * CHUNKS[1][1], 2 * CHUNKS[0][1])[c]
                if not isinstance(value, int) or value > 0:
                    act.wait_ge(dense_done, value)

            def split_weights_hi(s, k):
                if isinstance(s, int) and s < 2:
                    act.wait_ge(in_added, 12 * s + 3 * k + 3)
                else:
                    act.wait_ge(raw_loaded[k], 16 * (s + 1))
                if not (isinstance(s, int) and s == 0):
                    act.wait_ge(dense_done, GROUPS * s)
                nc.scalar.activation(w_hi[:, k, :], w_raw[:, k, :], ACT.Copy).then_inc(w_hi_ready, 1)

            def fronts(s):
                for c in range(3):
                    for f in range(KT):
                        unit = KT * c + f
                        if f == 0:
                            pt_slot_free(s, c)
                        act.wait_ge(front_done, FRONTS * s + unit + 1)
                        nc.scalar.activation(pt_hi[c % 2][:, f, 0:WIDTH[c]], front_bank[unit % 3][:, 0:WIDTH[c]], ACT.Copy).then_inc(front_hi, 1)
                        if c == 0:
                            split_weights_hi(s, f)

            def root_of_variance(m, n):
                act.wait_ge(moments_ready, TILES * m + n + 1)
                nc.scalar.activation(std[0:ROWS[n], n:n + 1], moments[0:ROWS[n], n, 1:2], ACT.Sqrt, bias=eps[0:ROWS[n], :]).then_inc(std_ready, 1)

            def source_tile(v, n, m=None, e=None):
                name, half, from_acc, norm = SOURCES[v]
                r, count = ROWS[n], TILES * v + n + 1
                if from_acc:
                    s_in = acc[0:r, n, 0:HALF]
                    if e == 1:
                        act.wait_ge(tail_done, TILES * TAILS[1] + n + 1)
                    if e == 4:
                        act.wait_ge(acc_done, GROUPS * EPOCHS[4][0] + 2 * (n + 1))
                else:
                    u = ROW_AT["source", v, n]
                    s_in = rows[0:r, u % 2, 0:HALF]
                    act.wait_ge(rows_loaded[u % 2], 16 * (u // 2 + 1))
                if count > 2:
                    act.wait_ge(h_ready, count - 2)
                if m is not None:
                    act.wait_ge(norm_ready, TILES * m + n + 1)
                t = t_buf[0:r, n % 2, :]
                if norm:
                    nc.scalar.activation(t, s_in, ACT.Relu, scale=scale[0:r, n:n + 1], bias=shift[0:r, n:n + 1]).then_inc(t_ready, 1)
                else:
                    nc.scalar.activation(t, s_in, ACT.Copy).then_inc(t_ready, 1)
                if v and n == 0:
                    act.wait_ge(front_done, FRONTS * (LAST_USE[v - 1] + 1))
                act.wait_ge(t_ready, count)
                nc.scalar.activation(h_hi[0:r, n, :], t, ACT.Copy).then_inc(h_hi_ready, 1)

            def sources_after(s):
                v = STEPS[s + 1][1]
                if FIRST_USE[v] != s + 1:
                    return
                e = EPOCH_END.get(s)
                boundary(v, e)

            def boundary(v, e):
                m = MOMENTS.get(e) if e is not None else None
                if m is not None:
                    for n in range(TILES):
                        root_of_variance(m, n)
                        if n:
                            source_tile(v, n - 1, m, e)
                    source_tile(v, TILES - 1, m, e)
                else:
                    for n in range(TILES):
                        source_tile(v, n, None, e)

            for k in range(2):
                with act.Fori(0, QUADS // 2) as i:
                    for b in range(2):
                        q = 2 * i + b
                        act.wait_ge(keys_ready, 1)
                        act.wait_ge(cast_done, 1 + 2 * i + k * QUADS)
                        for j in range(4):
                            last = nc.scalar.activation(diag[:, b, j, :], ident_f[:, :], ACT.Copy, scale=key[k][:, bass.ds(4 * q + j, 1)])
                        last.then_inc(diag_ready, 1)
                if k == 0:
                    boundary(0, -1)
            s = 0
            while s < len(STEPS):
                if STEPS[s][2] == "rel":
                    with act.Fori(0, RELATIONS) as r:
                        fronts(s + r)
                    s += RELATIONS
                else:
                    fronts(s)
                    if s == SUM_AFTER:
                        for n in range(TILES):
                            act.wait_ge(in_added, 24 + 3 * n + 3)
                            act.dma_start(asum[P * n:P * n + P, :], sum_buf[:, n % 2, :].bitcast(FP32)).then_inc(counts_stored[n % 2], 16)
                            if n:
                                store_self(act, n - 1)
                        store_self(act, TILES - 1)
                        act.wait_ge(deg_used, 1)
                        nc.scalar.activation(deg_std[:, :], deg_std[:, :], ACT.Sqrt).then_inc(deg_root, 1)
                    s += 1
                if s < len(STEPS):
                    sources_after(s - 1)
            e = len(EPOCHS) - 1
            for n in range(TILES):
                r, u = ROWS[n], ROW_AT["rest", e, n]
                act.wait_ge(rows_loaded[u % 2], 16 * (u // 2 + 1))
                if n >= 2:
                    act.wait_ge(out_ready, n - 1)
                nc.scalar.activation(w_raw[0:r, 2 + n % 2, :], rows[0:r, u % 2, :], ACT.Relu, scale=scale[0:r, n:n + 1], bias=shift[0:r, n:n + 1])
                act.wait_ge(u_loaded[n % 2], 16 * (n // 2 + 1))
                nc.scalar.activation(w_raw[0:r, n % 2, :], w_raw[0:r, n % 2, :], ACT.Tanh).then_inc(gate_act, 1)

        @block.tensor
        def _(pe):
            def mm(o, l, r, start, stop, **kw):
                return nc.tensor.matmul(o, l, r, start=start, stop=stop, **kw)

            for k in range(2):
                with pe.Fori(0, QUADS // 2) as i:
                    done = 2 * i + k * QUADS
                    for b in range(2):
                        q = done + b
                        pe.wait_ge(diag_ready, q + 1)
                        pe.wait_ge(same_ready, 1 + done)
                        mm(cast_bank[b][:, :], ones_f[:, :], diag[:, b, :, :].rearrange("p j c -> p (j c)"), True, True).then_inc(cast_done, 1)
                    for b in range(2):
                        q = done + b
                        pe.wait_ge(same_ready, 1 + q + 1)
                        pe.wait_ge(idx_ready, 1 + done)
                        for j in range(4):
                            mm(stat_bank[b][:, 3 * j:3 * j + 2], same[:, b, j, :], one_w[:, bass.ds(8 * (2 * i + b) + 2 * j, 2)], True, True)
                            last = mm(stat_bank[b][:, 3 * j + 2:3 * j + 3], before[:, b, j, :], ones_f[:, 0:1], True, True)
                        last.then_inc(stat_done, 1)

            def counts_loaded(c, g):
                pe.wait_ge(a_loaded[c % 2], 16 * (g + 1) if c == 1 else 16 * (2 * g + 1 + c // 2))

            def front(s, c, graph, v, g):
                a, b = CHUNKS[c]
                for f in range(KT):
                    unit = KT * c + f
                    cols = slice(P * f, P * f + P)
                    bank = front_bank[unit % 3]
                    if f == 0 and graph:
                        if c == 0:
                            pe.wait_ge(h_ready, TILES * (v + 1))
                        counts_loaded(c, g)
                    if not isinstance(s, int) or s or unit >= 3:
                        pe.wait_ge(front_lo, FRONTS * s + unit - 2)
                    if graph:
                        for n in range(TILES):
                            k = ROWS[n]
                            counts = a_chunk[c % 2][0:k, n, 0:WIDTH[c]]
                            mm(bank[:, 0:WIDTH[c]], h_hi[0:k, n, cols], counts, n == 0, False)
                            last = mm(bank[:, 0:WIDTH[c]], h_lo[0:k, n, cols], counts, False, n == TILES - 1)
                    else:
                        for n in range(a, b):
                            if f == 0:
                                pe.wait_ge(h_ready, TILES * v + n + 1)
                            k, o = ROWS[n], P * (n - a)
                            mm(bank[:, o:o + k], h_hi[0:k, n, cols], ident[0:k, 0:k], True, False)
                            last = mm(bank[:, o:o + k], h_lo[0:k, n, cols], ident[0:k, 0:k], False, True)
                    last.then_inc(front_done, 1)

            def degrees(r, c, g):
                counts_loaded(c, g)
                pe.wait_ge(deg_used, 1 + 3 * r + c)
                for n in range(*CHUNKS[c]):
                    o = P * (n - CHUNKS[c][0])
                    for j in range(TILES):
                        last = mm(deg_bank[0:ROWS[n], 2 * n:2 * n + 2], a_chunk[c % 2][0:ROWS[j], j, o:o + ROWS[n]],
                                  ones2[0:ROWS[j], :], j == 0, j == TILES - 1)
                last.then_inc(deg_done, 1)

            def dense(s, c):
                if c == 0:
                    pe.wait_ge(w_lo_ready, KT * (s + 1))
                pe.wait_ge(front_lo, FRONTS * s + KT * (c + 1))
                for n in range(*CHUNKS[c]):
                    m, o = ROWS[n], P * (n - CHUNKS[c][0])
                    for half in range(2):
                        group = 2 * n + half
                        if not isinstance(s, int) or s or group >= 4:
                            pe.wait_ge(acc_done, GROUPS * s + group - 3)
                        bank = dense_bank[group % 4][0:m, :]
                        cols = slice(512 * half, 512 * half + 512)
                        for f in range(KT):
                            hi, lo = pt_hi[c % 2][:, f, o:o + m], pt_lo[c % 2][:, f, o:o + m]
                            mm(bank, hi, w_hi[:, f, cols], f == 0, False)
                            mm(bank, hi, w_lo[:, f, cols], False, False)
                            last = mm(bank, lo, w_hi[:, f, cols], False, f == KT - 1)
                        last.then_inc(dense_done, 1)

            def step(s, graph, v, g, r=None):
                for c in range(2):
                    if r is not None:
                        degrees(r, c, g)
                    front(s, c, graph, v, g)
                dense(s, 0)
                if r is not None:
                    degrees(r, 2, g)
                front(s, 2, graph, v, g)
                dense(s, 1)
                dense(s, 2)

            s = 0
            while s < len(STEPS):
                graph, v, name, half = STEPS[s]
                g = G_BEFORE[s]
                if name == "rel":
                    with pe.Fori(0, RELATIONS) as r:
                        step(s + r, graph, v, g + r, r if half == 0 else None)
                    s += RELATIONS
                    continue
                step(s, graph, v, g)
                if s == SUM_AFTER:
                    for n in range(TILES):
                        pe.wait_ge(in_added, 24 + 3 * n + 3)
                        for d in range(TILES):
                            last = mm(deg_bank[0:ROWS[d], 2 * d:2 * d + 2], sum_buf[:, n % 2, P * d:P * d + ROWS[d]], ones2[:, :],
                                      n == 0 and d == 0, n == TILES - 1, skip_group_check=True)
                        last.then_inc(deg_piece, 1)
                s += 1

        @block.vector
        def _(dve):
            V = nc.vector
            count = [0]

            def link(ins):
                count[0] += 1
                ins.then_inc(small, 1)
                dve.wait_ge(small, count[0])

            dve.wait_ge(consts, 7)
            V.tensor_copy(ident[:, :], ident_f[:, :])
            V.tensor_copy(ones2[:, :], ones_f[:, 0:2])
            V.memset(deg_inv[:, :], 1.0).then_inc(cast_done, 1)
            V.memset(deg_std[:, :], 1.0).then_inc(same_ready, 1)
            V.memset(rel_inv[:, :], 1.0).then_inc(stat_done, 1)
            V.memset(std[:, :], 1.0).then_inc(idx_ready, 1)
            link(V.tensor_copy(trash["w"][:, :], trash_i[:, :]))
            V.tensor_scalar(trash["a"][:, :], trash["w"][:, :], float(NA), None, ALU.add)
            V.tensor_scalar(trash["r"][:, :], trash["w"][:, :], float(RELATIONS * NA), None, ALU.add)
            dve.wait_ge(edges_in, 64)
            link(V.tensor_copy(edges_f[:, :, :], edges_i[:, :, :]))
            link(V.tensor_scalar(trash["w"][:, :], trash["w"][:, :], float(NW), None, ALU.add))
            src_f, dst_f, type_f = (edges_f[:, i, :] for i in range(3))
            ones_w = one_w[:, :].rearrange("p (t c) -> p t c", c=2)
            V.memset(ones_w[:, :, 0:1], 1.0)
            V.tensor_copy(ones_w[:, :, 1:2], edge_w[:, :, None])
            V.scalar_tensor_tensor(out=key_w[:, :], in0=dst_f, scalar=float(FEATURES), in1=src_f, op0=ALU.mult, op1=ALU.add)
            V.scalar_tensor_tensor(out=key[0][:, :], in0=src_f, scalar=float(NODES), in1=dst_f, op0=ALU.mult, op1=ALU.add)
            V.scalar_tensor_tensor(out=src_row[:, :], in0=type_f, scalar=float(PADDED), in1=src_f, op0=ALU.mult, op1=ALU.add)
            V.tensor_scalar(valid[:, 0, :], src_f, float(FEATURES), None, ALU.is_lt)
            link(V.tensor_scalar(valid[:, 1, :], src_f, float(NODES), None, ALU.is_lt))
            V.scalar_tensor_tensor(out=key[1][:, :], in0=src_row[:, :], scalar=float(NODES), in1=dst_f, op0=ALU.mult, op1=ALU.add)
            link(V.scalar_tensor_tensor(out=valid[:, 0, :], in0=dst_f, scalar=float(FEATURES), in1=valid[:, 0, :], op0=ALU.is_lt, op1=ALU.mult))
            for name, k, ok in (("w", key_w, 0), ("a", key[0], 1), ("r", key[1], 1)):
                last = V.scalar_tensor_tensor(out=off[name][:, :], in0=k[:, :], scalar=trash[name][:, 0:1], in1=valid[:, ok, :],
                                              op0=ALU.subtract, op1=ALU.mult)
            last.then_inc(keys_ready, 1)
            dve.wait_ge(keys_ready, 1)

            def compare(k):
                with dve.Fori(0, QUADS // 2) as i:
                    done = 2 * i + k * QUADS
                    for b in range(2):
                        q, cols = done + b, bass.ds(4 * (2 * i + b), 4)
                        dve.wait_ge(cast_done, 1 + q + 1)
                        dve.wait_ge(stat_done, 1 + done)
                        V.tensor_tensor(same[:, b, :, :], cast_bank[b][:, :].rearrange("p (j c) -> p j c", c=P),
                                        key[k][:, cols].unsqueeze(2).to_broadcast((P, 4, P)),
                                        ALU.is_equal).then_inc(equal_done, 1)
                        dve.wait_ge(equal_done, q + 1)
                        V.tensor_tensor(before[:, b, :, :], same[:, b, :, :], below[:, :].unsqueeze(1).to_broadcast((P, 4, P)),
                                        ALU.mult).then_inc(same_ready, 1)
                    for b in range(2):
                        q, cols = done + b, bass.ds(4 * (2 * i + b), 4)
                        dve.wait_ge(stat_done, 1 + q + 1)
                        sums = stat_bank[b][:, 0:12].rearrange("p (j c) -> p j c", c=3)
                        names = "wa" if k == 0 else "r"
                        for m, name in enumerate(names):
                            last = V.scalar_tensor_tensor(out=idx_f[:, b, m, :], in0=sums[:, :, 2], scalar=0.5, in1=off[name][:, cols],
                                                          op0=ALU.is_lt, op1=ALU.mult)
                        last.then_inc(row_done, 1)
                        if k == 0:
                            V.tensor_copy(wsum[:, cols], sums[:, :, 1])
                        V.tensor_copy((cnt_a if k == 0 else cnt_r)[:, cols], sums[:, :, 0])
                        dve.wait_ge(row_done, q + 1)
                        for m, name in enumerate(names):
                            last = V.tensor_scalar({"w": idx_w, "a": idx_a, "r": idx_r}[name][:, cols], idx_f[:, b, m, :],
                                                   trash[name][:, 0:1], None, ALU.add)
                        last.then_inc(idx_ready, 1)

            def take_moments(m, n):
                r = ROWS[n]
                if TILES * m + n >= 2:
                    dve.wait_ge(moments_ready, TILES * m + n - 1)
                for i in range(2):
                    last = V.bn_stats(partial[0:r, n % 2, i, :], acc[0:r, n, HALF * i:HALF * (i + 1)])
                link(last)
                V.bn_aggr(moments[0:r, n, :], partial[0:r, n % 2, :, :].rearrange("p a b -> p (a b)")).then_inc(moments_ready, 1)

            def take_norm(m, n, e):
                r, c = ROWS[n], slice(n, n + 1)
                dve.wait_ge(std_ready, TILES * m + n + 1)
                link(V.reciprocal(scale[0:r, c], std[0:r, c]))
                if e == 2:
                    link(V.tensor_tensor(scale[0:r, c], scale[0:r, c], dinv[0:r, c], ALU.mult))
                V.scalar_tensor_tensor(out=shift[0:r, c], in0=moments[0:r, n, 0:1], scalar=-1.0, in1=scale[0:r, c],
                                       op0=ALU.mult, op1=ALU.mult).then_inc(norm_ready, 1)

            def source_lo(v, n):
                r = ROWS[n]
                dve.wait_ge(h_hi_ready, TILES * v + n + 1)
                V.tensor_tensor(h_lo[0:r, n, :], t_buf[0:r, n % 2, :], h_hi[0:r, n, :].bitcast(FP32), ALU.subtract).then_inc(h_ready, 1)

            def tail(e, n):
                last, how, _, _, _, _ = EPOCHS[e]
                r = ROWS[n]
                dve.wait_ge(acc_done, GROUPS * last + 2 * (n + 1))
                if how == "relu":
                    V.tensor_scalar(acc[0:r, n, :], acc[0:r, n, :], 0.0, None, ALU.max).then_inc(tail_done, 1)
                    return
                u = ROW_AT["rest", e, n]
                dve.wait_ge(rows_loaded[u % 2], 16 * (u // 2 + 1))
                rest = rows[0:r, u % 2, :]
                if how == "add":
                    V.tensor_tensor(acc[0:r, n, :], acc[0:r, n, :], rest, ALU.add).then_inc(tail_done, 1)
                else:
                    V.scalar_tensor_tensor(out=acc[0:r, n, :], in0=acc[0:r, n, :], scalar=0.0, in1=rest, op0=ALU.max, op1=ALU.add).then_inc(tail_done, 1)
                dve.wait_ge(tail_done, TILES * TAILS[e] + n + 1)

            def final(n):
                r, u = ROWS[n], ROW_AT["rest", len(EPOCHS) - 1, n]
                th, h3, x3, z = w_raw[0:r, n % 2, :], w_raw[0:r, 2 + n % 2, :], rows[0:r, u % 2, :], acc[0:r, n, :]
                dve.wait_ge(gate_act, n + 1)
                link(V.tensor_tensor(th, th, h3, ALU.subtract))
                dve.wait_ge(acc_done, GROUPS * LAST + 2 * (n + 1))
                V.tensor_tensor(h3, h3, x3, ALU.add)
                link(V.tensor_tensor(th, th, z, ALU.mult))
                V.tensor_tensor(z, th, h3, ALU.add).then_inc(out_ready, 1)

            def after_step(s):
                jobs = [[] for _ in range(13)]
                if s == LAST:
                    for n in range(TILES):
                        jobs[n if n < 8 else 2 * n - 7].append(lambda n=n: final(n))
                    return jobs
                v = STEPS[s + 1][1]
                if FIRST_USE[v] != s + 1:
                    return jobs
                e = EPOCH_END.get(s)
                for n in range(TILES):
                    slot = n if n < 8 or e is None else 2 * n - 7
                    if e is None:
                        jobs[slot].append(lambda n=n: source_lo(v, n))
                        continue
                    if EPOCHS[e][1] != "none":
                        jobs[slot].append(lambda n=n: tail(e, n))
                    if EPOCHS[e][5]:
                        m = MOMENTS[e]
                        jobs[slot].append(lambda n=n: take_moments(m, n))
                        if n:
                            jobs[slot].append(lambda n=n: take_norm(m, n - 1, e))
                        if n > 1:
                            jobs[slot].append(lambda n=n: source_lo(v, n - 2))
                    elif n:
                        jobs[slot].append(lambda n=n: source_lo(v, n - 1))
                if e is not None:
                    if EPOCHS[e][5]:
                        jobs[12] += [lambda: take_norm(MOMENTS[e], TILES - 1, e), lambda: source_lo(v, TILES - 2)]
                    jobs[12].append(lambda: source_lo(v, TILES - 1))
                return jobs

            def add_table(q, into, out_ap, width, loaded, value):
                dve.wait_ge(in_loaded[q % 5], 16 * (q // 5 + 1))
                dve.wait_ge(loaded, value)
                if q:
                    dve.wait_ge(in_added, q)
                V.tensor_tensor(out_ap, into, in_buf[:, q % 5, 0:width], ALU.add).then_inc(in_added, 1)

            def add_edge_weights(s):
                for k in range(KT):
                    for j in range(TABLES - 1):
                        add_table(12 * s + 3 * k + j, w_raw[:, k, :], w_raw[:, k, :], FEATURES, raw_loaded[k], 16 * (s + 1))

            def add_counts():
                def self_loops(n):
                    w = ROWS[n]
                    dve.wait_ge(deg_piece, n + 1)
                    dve.wait_ge(counts_stored[n % 2], 16 * (n // 2 + 1))
                    block_n = sum_buf[:, n % 2, P * n:P * n + w]
                    V.tensor_tensor(block_n, block_n.bitcast(FP32), ident[:, 0:w].bitcast(FP32), ALU.add).then_inc(self_added, 1)

                for n in range(TILES):
                    for j in range(TABLES - 1):
                        part = sum_buf[:, n % 2, :]
                        add_table(24 + 3 * n + j, part.bitcast(FP32), part, NODES, t0_loaded[n % 2], 16 * (n // 2 + 1))
                    if n:
                        self_loops(n - 1)
                self_loops(TILES - 1)
                deg = deg_bank[:, 0:2 * TILES].rearrange("p (n c) -> p n c", c=2)[:, :, 0]
                for r, c in ((P, slice(0, TILES - 1)), (ROWS[-1], slice(TILES - 1, TILES))):
                    V.tensor_scalar(deg_inv[0:r, c], deg[0:r, c], 1.0, None, ALU.max)
                    last = V.tensor_scalar(deg_std[0:r, c], deg[0:r, c], 1.0, None, ALU.add)
                last.then_inc(deg_used, 1)
                dve.wait_ge(deg_used, 1)
                V.reciprocal(deg_inv[:, :], deg_inv[:, :])
                dve.wait_ge(deg_root, 1)
                link(V.reciprocal(dinv[:, :], deg_std[:, :]))

            def relation_degrees(r, c):
                dve.wait_ge(deg_done, 3 * r + c + 1)
                a, b = CHUNKS[c]
                deg = deg_bank[:, 0:2 * TILES].rearrange("p (n c) -> p n c", c=2)[:, :, 0]
                whole = min(b, TILES - 1)
                last = V.tensor_scalar(deg_std[:, a:whole], deg[:, a:whole], 1.0, None, ALU.max)
                if b == TILES:
                    last = V.tensor_scalar(deg_std[0:ROWS[-1], b - 1:b], deg[0:ROWS[-1], b - 1:b], 1.0, None, ALU.max)
                last.then_inc(deg_used, 1)
                dve.wait_ge(deg_used, 1 + 3 * r + c + 1)
                V.reciprocal(rel_inv[:, bass.ds(TILES * r + a, b - a)], deg_std[:, a:b]).then_inc(deg_small, 1)
                dve.wait_ge(deg_small, 3 * r + c + 1)

            def step(s, graph, name, half, r=None, jobs=None):
                def low_part(unit):
                    c, f = divmod(unit, KT)
                    dve.wait_ge(front_hi, FRONTS * s + unit + 1)
                    V.tensor_tensor(pt_lo[c % 2][:, f, 0:WIDTH[c]], front_bank[unit % 3][:, 0:WIDTH[c]],
                                    pt_hi[c % 2][:, f, 0:WIDTH[c]].bitcast(FP32), ALU.subtract).then_inc(front_lo, 1)

                def add_group(group):
                    n, o = divmod(group, 2)
                    m = ROWS[n]
                    dve.wait_ge(dense_done, GROUPS * s + group + 1)
                    tile = acc[0:m, n, 512 * o:512 * o + 512]
                    bank = dense_bank[group % 4][0:m, :]
                    if graph:
                        by = rel_inv[0:m, bass.ds(TILES * r + n, 1)] if r is not None else (dinv if name == "gcn" else deg_inv)[0:m, n:n + 1]
                        V.scalar_tensor_tensor(out=tile, in0=bank, scalar=by, in1=tile, op0=ALU.mult, op1=ALU.add).then_inc(acc_done, 1)
                    else:
                        V.tensor_tensor(tile, bank, tile, ALU.add).then_inc(acc_done, 1)

                if name == "edge":
                    add_edge_weights(s)
                for f in range(KT):
                    low_part(f)
                    dve.wait_ge(w_hi_ready, KT * s + f + 1)
                    V.tensor_tensor(w_lo[:, f, :], w_raw[:, f, :], w_hi[:, f, :].bitcast(FP32), ALU.subtract).then_inc(w_lo_ready, 1)
                if name == "rel" and half == 0:
                    relation_degrees(r, 0)
                for f in range(KT):
                    low_part(KT + f)
                if name == "rel" and half == 0:
                    relation_degrees(r, 1)
                if isinstance(s, int) and (s == 0 or s - 1 in EPOCH_END):
                    epoch = 0 if s == 0 else EPOCH_END[s - 1] + 1
                    dve.wait_ge(acc_set, 16 * TILES * (epoch + 1))
                for group in range(2 * CHUNKS[0][1]):
                    add_group(group)
                for f in range(KT):
                    low_part(2 * KT + f)
                if name == "rel" and half == 0:
                    relation_degrees(r, 2)
                for slot, group in enumerate(range(2 * CHUNKS[0][1], GROUPS)):
                    add_group(group)
                    for job in (jobs[slot] if jobs else ()):
                        job()
                for job in (jobs[12] if jobs else ()):
                    job()

            compare(0)
            dve.wait_ge(x_in, 32)
            for n in range(TILES):
                take_moments(0, n)
                if n:
                    take_norm(0, n - 1, -1)
                if n > 1:
                    source_lo(0, n - 2)
            take_norm(0, TILES - 1, -1)
            source_lo(0, TILES - 2)
            source_lo(0, TILES - 1)
            compare(1)
            s = 0
            while s < len(STEPS):
                graph, v, name, half = STEPS[s]
                if name == "rel":
                    with dve.Fori(0, RELATIONS - 1) as r:
                        step(s + r, graph, name, half, r)
                    s += RELATIONS
                    step(s - 1, graph, name, half, RELATIONS - 1, after_step(s - 1))
                    continue
                step(s, graph, name, half, None, after_step(s))
                if s == SUM_AFTER:
                    add_counts()
                s += 1


_INPUTS = ["x", "src", "dst", "edge_type_8", "edge_weight", "L0_gnn_bias", "L1_gnn_W_self0", "L1_gnn_W_neigh0", "L1_gnn_b0",
           "L1_gnn_W_self1", "L1_gnn_W_neigh1", "L1_gnn_b1", "L2_gnn_W", "L2_gnn_b", "L3_gnn_weight", "L3_gnn_root",
           "L3_gnn_bias", "L3_gnn_w_gate", "L3_gnn_b_gate"]


def kernel(**inputs):
    import numpy as _np
    import concourse.bacc as _bacc
    from concourse import mybir as _mybir
    from concourse.bass_utils import run_bass_kernel_spmd as _run

    nc = _bacc.Bacc("TRN2", target_bir_lowering=False, num_devices=1)
    arrays, args = {}, []
    for name in _INPUTS:
        a = _np.ascontiguousarray(inputs[name])
        arrays[f"in_{name}"] = a
        args.append(nc.dram_tensor(f"in_{name}", a.shape, _mybir.dt.from_np(a.dtype), kind="ExternalInput").ap())
    out = nc.dram_tensor("out_0", (NODES, FEATURES), FP32, kind="ExternalOutput").ap()
    build(nc, *args, out)
    r = _run(nc, [arrays], core_ids=[0])
    return r.results[0]["out_0"]
```

```python
import concourse.bass as bass
from concourse import mybir
from contextlib import ExitStack

FP32 = mybir.dt.float32
F32R = mybir.dt.float32r
BF16 = mybir.dt.bfloat16
I32 = mybir.dt.int32
ALU = mybir.AluOpType
ACT = mybir.ActivationFunctionType

P = 128
NODES = 1250
FEATURES = 1024
EDGES = 20000
RELATIONS = 8
HALF = FEATURES // 2
KT = HALF // P
TILES = -(-NODES // P)
ROWS = [min(P, NODES - P * n) for n in range(TILES)]
PADDED = TILES * P
CHUNKS = [(0, 4), (4, 7), (7, 10)]
WIDTH = [sum(ROWS[a:b]) for a, b in CHUNKS]
START = [P * a for a, _ in CHUNKS]
GROUPS = 2 * TILES
FRONTS = KT * len(CHUNKS)
EDGE_ROWS = 125
EDGE_COLS = EDGES // EDGE_ROWS
QUADS = EDGE_COLS // 4
TABLES = 2
SPARE = 4 * P
ZERO_PIECES = 10 * RELATIONS
NW = FEATURES * FEATURES
NA = PADDED * NODES
EPS = 1e-5

SOURCES = [("x", 0, True, True), ("x", 1, False, True),
           ("x1", 0, True, True), ("x1", 1, False, True), ("x1", 0, False, True),
           ("g", 0, True, False), ("g", 1, False, False),
           ("x2", 0, True, True), ("x2", 1, False, True),
           ("x3", 0, True, True), ("x3", 1, False, True),
           ("u", 0, True, False), ("u", 1, False, False),
           ("x3", 0, False, True), ("x3", 1, False, True)]
STEPS = [(False, 0, "edge", 0), (False, 1, "edge", 1),
         (False, 2, "self0", 0), (False, 3, "self0", 1), (True, 3, "neigh0", 1), (True, 4, "neigh0", 0),
         (False, 5, "self1", 0), (True, 5, "neigh1", 0), (False, 6, "self1", 1), (True, 6, "neigh1", 1),
         (True, 7, "gcn", 0), (True, 8, "gcn", 1),
         (False, 9, "root", 0)] + [(True, 9, "rel", 0)] * RELATIONS + [
         (False, 10, "root", 1)] + [(True, 10, "rel", 1)] * RELATIONS + [
         (False, 11, "gate", 0), (False, 12, "gate", 1), (False, 13, "gate", 2), (False, 14, "gate", 3)]
G_BEFORE = [sum(t[0] for t in STEPS[:s]) for s in range(len(STEPS))]
LAST = len(STEPS) - 1
FIRST_SELF = G_BEFORE[[t[2] for t in STEPS].index("gcn")]
EPOCHS = [(1, "add", "x1", "x", "b0", True), (5, "relu", "g", None, "b10", False),
          (9, "add", "x2", "x1", "b11", True), (11, "relu_add", "x3", "x2", "b2", True),
          (29, "none", "u", None, "b3", False), (LAST, "gate", "out", "x3", "bg", False)]
EPOCH_END = {e[0]: n for n, e in enumerate(EPOCHS)}
LAST_USE = [max(s for s, t in enumerate(STEPS) if t[1] == v) for v in range(len(SOURCES))]
FIRST_USE = [min(s for s, t in enumerate(STEPS) if t[1] == v) for v in range(len(SOURCES))]
FIRST_GRAPH = min(s for s, t in enumerate(STEPS) if t[0])
MOMENTS = {-1: 0, 0: 1, 2: 2, 3: 3}
TAILS = {0: 0, 1: 1, 2: 2, 3: 3}

WSUM = KT * (TABLES - 1)
ZERO_BY_ACT = 4 * FRONTS
ROW_USES = []
for _v, (_, _, _from_acc, _) in enumerate(SOURCES):
    for _e, _ep in enumerate(EPOCHS[:-1]):
        if FIRST_USE[_v] == _ep[0] + 1 and _ep[3]:
            ROW_USES += [("rest", _e, n) for n in range(TILES)]
    if not _from_acc:
        ROW_USES += [("source", _v, n) for n in range(TILES)]
ROW_USES += [("rest", len(EPOCHS) - 1, n) for n in range(TILES)]
ROW_AT = {u: i for i, u in enumerate(ROW_USES)}


def build(nc, x, src, dst, etype, eweight, b0, self0, neigh0, b10, self1, neigh1, b11, gcn, b2, rel,
          root, b3, gate, bg, out):
    def dram(name, shape):
        return nc.dram_tensor(name, shape, FP32, kind="Internal").ap()

    wtab = [dram(f"wtab{j}", (NW + SPARE, 1)) for j in range(TABLES)]
    atab = dram("atab", (NA + SPARE, 1))
    rtab = dram("rtab", (RELATIONS * NA + SPARE, 1))
    rows_of = {"x": x, "out": out}
    for name in ("x1", "x2", "x3", "g", "u"):
        rows_of[name] = dram(name, (NODES, FEATURES))
    weights = {"self0": self0, "neigh0": neigh0, "self1": self1, "neigh1": neigh1, "gcn": gcn,
               "root": root, "gate": gate, "rel": rel.rearrange("r k o -> (r k) o")}
    bias = {"b0": b0, "b10": b10, "b11": b11, "b2": b2, "b3": b3, "bg": bg}
    wtab2 = [t[0:NW].rearrange("(d s) c -> d (s c)", s=FEATURES) for t in wtab]
    atab2 = atab[0:NA].rearrange("(s d) c -> s (d c)", d=NODES)
    rtab2 = rtab[0:RELATIONS * NA].rearrange("(s d) c -> s (d c)", d=NODES)

    ctx = ExitStack()
    with ctx:
        base = nc.sbuf_base
        arena = ctx.enter_context(nc.sbuf_tensor("arena", [P, 212768], mybir.dt.uint8))
        top = [-(-base // 32) * 32]

        def place(name, shape, dt, at=None):
            size = 2 if dt == BF16 else 4
            for d in shape[1:]:
                size *= d
            if at is None:
                at = top[0]
                top[0] = -(-(at + size) // 32) * 32
                assert top[0] <= base + 212768, (name, top[0] - base)
            return nc.alloc_sbuf_tensor_at(name, shape, dt, offset=at)

        def sem(name):
            return ctx.enter_context(nc.semaphore(name))

        h_hi = place("h_hi", [P, TILES, HALF], F32R)
        h_lo = place("h_lo", [P, TILES, HALF], F32R)
        pt_hi_at = top[0]
        pt_hi = [place(f"pt_hi{i}", [P, KT, WIDTH[i]], F32R) for i in range(2)]
        pt_lo = [place(f"pt_lo{i}", [P, KT, WIDTH[i]], F32R) for i in range(2)]
        w_raw = place("w_raw", [P, KT, FEATURES], FP32)
        w_hi = place("w_hi", [P, KT, FEATURES], F32R)
        w_lo = place("w_lo", [P, KT, FEATURES], F32R)
        acc = place("acc", [P, TILES, FEATURES], FP32)
        counts_at = top[0]
        a_chunk = [place(f"a_chunk{i}", [P, TILES, WIDTH[i]], F32R) for i in range(2)]
        rows = place("rows", [P, 2, FEATURES], FP32)
        t_buf = place("t_buf", [P, 2, HALF], FP32)
        ident_wide = place("ident_wide", [P, 3 * P], F32R)
        ident = ident_wide[:, P:2 * P]
        ones = place("ones", [P, P], F32R)
        idx_r = place("idx_r", [P, EDGE_COLS], I32)
        cnt_r = place("cnt_r", [P, EDGE_COLS], FP32)
        idx_slot = place("idx_slot", [P, 2, 4], I32)
        val_slot = place("val_slot", [P, 2, 4], FP32)
        moments = place("moments", [P, TILES, 2], FP32)
        partial = place("partial", [P, 2, 2, 6], FP32)
        std = place("std", [P, TILES], FP32)
        scale = place("scale", [P, TILES], FP32)
        shift = place("shift", [P, TILES], FP32)
        deg_inv = place("deg_inv", [P, TILES], FP32)
        deg_std = place("deg_std", [P, TILES], FP32)
        dinv = place("dinv", [P, TILES], FP32)
        rel_inv = place("rel_inv", [P, RELATIONS * TILES], FP32)
        eps = place("eps", [P, 1], FP32)
        in_buf = place("in_buf", [P, WSUM, FEATURES], FP32, counts_at)
        late_at = counts_at + 27200
        at = [counts_at]

        def prep(name, shape, dt):
            size = 2 if dt == BF16 else 4
            for d in shape[1:]:
                size *= d
            t = place(name, shape, dt, at[0])
            at[0] += -(-size // 32) * 32
            return t

        same = prep("same", [P, 2, 4, 4 * P], BF16)
        before = prep("before", [P, 2, 4, P], BF16)
        ident_f = prep("ident_f", [P, P], FP32)
        ones_f = prep("ones_f", [P, P], FP32)
        below = prep("below", [P, P], BF16)
        idx_w = prep("idx_w", [P, EDGE_COLS], I32)
        wsum = prep("wsum", [P, EDGE_COLS], FP32)
        key = [prep(f"key{i}", [P, EDGE_COLS], FP32) for i in range(2)]
        off = {name: prep(f"off_{name}", [P, EDGE_COLS], FP32) for name in "war"}
        values = prep("values", [P, 10 * EDGE_COLS], BF16)
        spare_i = prep("spare_i", [P, 4], I32)
        spare = {name: prep(f"spare_{name}", [P, 4], FP32) for name in "war"}
        idx_f = prep("idx_f", [P, 2, 2, 4], FP32)
        assert max(at[0], counts_at + WSUM * FEATURES * 4) <= late_at, at[0] - counts_at
        at[0] = late_at
        diag = place("diag", [P, 2, 4, P], FP32, pt_hi_at)
        key_row = place("key_row", [P, 2, 4 * P], FP32, pt_hi_at + 2 * 4 * P * 4)
        idx_a = prep("idx_a", [P, EDGE_COLS], I32)
        cnt_a = prep("cnt_a", [P, EDGE_COLS], FP32)
        zeros = prep("zeros", [P, NODES], FP32)
        assert at[0] <= counts_at + TILES * (WIDTH[0] + WIDTH[1]) * 4
        at[0] = -(-(base) // 32) * 32
        edges_i = prep("edges_i", [P, 3, EDGE_COLS], I32)
        edges_f = prep("edges_f", [P, 3, EDGE_COLS], FP32)
        edge_w = prep("edge_w", [P, EDGE_COLS], FP32)
        part = prep("part", [P, 3, EDGE_COLS], BF16)
        valid = prep("valid", [P, 2, EDGE_COLS], FP32)
        src_row = prep("src_row", [P, EDGE_COLS], FP32)
        key_w = prep("key_w", [P, EDGE_COLS], FP32)

        banks = [ctx.enter_context(nc.psum_tensor(f"bank{i}", [P, 512], FP32)) for i in range(8)]
        front_bank, dense_bank, deg_bank = banks[0:3], banks[3:7], banks[7]
        cast_bank, stat_bank = banks[3:5], banks[5:7]

        edges_in = sem("edges_in")
        x_in = sem("x_in")
        consts = sem("consts")
        small = sem("small")
        keys_ready = sem("keys_ready")
        equal_done = sem("equal_done")
        row_done = sem("row_done")
        zeroed = {name: sem(f"zeroed_{name}") for name in "war"}
        diag_ready = sem("diag_ready")
        cast_done = sem("cast_done")
        row_ready = sem("row_ready")
        same_ready = sem("same_ready")
        stat_done = sem("stat_done")
        idx_ready = sem("idx_ready")
        slot_ready = sem("slot_ready")
        added = {"w": [sem(f"added_w{j}") for j in range(TABLES)],
                 "a": [sem("added_a")], "r": [sem("added_r")]}
        in_loaded = [sem(f"in_loaded{i}") for i in range(WSUM)]
        in_added = sem("in_added")
        self_added = sem("self_added")
        raw_loaded = [sem(f"raw_loaded{k}") for k in range(KT)]
        w_hi_ready = sem("w_hi_ready")
        w_lo_ready = sem("w_lo_ready")
        a_loaded = [sem(f"a_loaded{i}") for i in range(2)]
        front_done = sem("front_done")
        front_hi = sem("front_hi")
        front_lo = sem("front_lo")
        dense_done = sem("dense_done")
        acc_done = sem("acc_done")
        deg_done = sem("deg_done")
        deg_used = sem("deg_used")
        deg_root = sem("deg_root")
        self_degrees = sem("self_degrees")
        deg_small = sem("deg_small")
        moments_ready = sem("moments_ready")
        std_ready = sem("std_ready")
        norm_ready = sem("norm_ready")
        tail_done = sem("tail_done")
        rows_loaded = [sem(f"rows_loaded{i}") for i in range(2)]
        u_loaded = [sem(f"u_loaded{i}") for i in range(2)]
        t_ready = sem("t_ready")
        h_hi_ready = sem("h_hi_ready")
        h_ready = sem("h_ready")
        stored = [sem(f"stored{i}") for i in range(2)]
        acc_set = sem("acc_set")
        gate_act = sem("gate_act")
        out_ready = sem("out_ready")

        block = ctx.enter_context(nc.Block())

        def row_free(use):
            kind, which, n = ROW_USES[use]
            if kind == "source":
                return t_ready, TILES * which + n + 1
            if which == len(EPOCHS) - 1:
                return out_ready, n + 1
            return tail_done, TILES * TAILS[which] + n + 1

        def zero_piece(eng, i):
            piece = rtab[i * P * NODES:(i + 1) * P * NODES].rearrange("(p w) o -> p (w o)", p=P)
            eng.dma_start(piece, zeros[:, :]).then_inc(zeroed["r"], 16)

        @block.sync
        def _(sp):
            sp.wait_ge(consts, 1)
            for i, a in enumerate((src, dst, etype)):
                sp.dma_start(edges_i[0:EDGE_ROWS, i, :], a.rearrange("(p t) -> p t", p=EDGE_ROWS)).then_inc(edges_in, 16)
            sp.dma_start(edge_w[0:EDGE_ROWS, :], eweight.rearrange("(p t) -> p t", p=EDGE_ROWS)).then_inc(edges_in, 16)
            sp.wait_ge(consts, 2)
            for name, tabs, n, width in (("w", wtab, NW, FEATURES), ("a", [atab], NA, NODES)):
                for tab in tabs:
                    piece = tab[0:n].rearrange("(p c w) o -> p c (w o)", p=P, w=width)
                    sp.dma_start(piece, zeros[:, None, 0:width].to_broadcast((P, piece.shape[1], width))).then_inc(zeroed[name], 16)
                if name == "w":
                    full = TILES - 1
                    sp.dma_start(acc[:, 0:full, :], x[0:full * P, :].rearrange("(n p) f -> p n f", p=P)).then_inc(x_in, 16)
                    sp.dma_start(acc[0:ROWS[full], full, :], x[full * P:, :]).then_inc(x_in, 16)
            for i in range(ZERO_PIECES - ZERO_BY_ACT):
                sp.wait_ge(added["w"][i % 2], 16 * (1 + 4 * (i // 2)))
                zero_piece(sp, i)

            def load_weights(s, first_row, name):
                for k in range(KT):
                    if k == 0 and not (isinstance(s, int) and s == 0):
                        sp.wait_ge(w_lo_ready, KT * s)
                    sp.dma_start(w_raw[:, k, :], weights[name][bass.ds(first_row + P * k, P), :]).then_inc(raw_loaded[k], 16)

            def load_in(q, src_ap):
                if q >= WSUM:
                    sp.wait_ge(in_added, q - WSUM + 1)
                sp.dma_start(in_buf[:, q % WSUM, :], src_ap).then_inc(in_loaded[q % WSUM], 16)

            def load_edge_weights(s):
                if s == 0:
                    sp.wait_ge(idx_ready, 2 + 2 * QUADS)
                    for j in range(TABLES):
                        sp.wait_ge(added["w"][j], 16 * (1 + 2 * QUADS))
                for k in range(KT):
                    d = HALF * s + P * k
                    if s and k == 0:
                        sp.wait_ge(w_lo_ready, KT * s)
                    sp.dma_start(w_raw[:, k, :], wtab2[0][d:d + P, :]).then_inc(raw_loaded[k], 16)
                    for j in range(1, TABLES):
                        load_in(WSUM * s + (TABLES - 1) * k + j - 1, wtab2[j][d:d + P, :])

            def load_counts(c, g, tab, first_row, fronts_then=None):
                cols = slice(START[c], START[c] + WIDTH[c])
                region = a_chunk[c % 2][:, :, 0:WIDTH[c]].bitcast(FP32)
                sp.wait_ge(added["r" if tab is rtab2 else "a"][0], 16 * (1 + EDGE_COLS))
                if fronts_then is not None:
                    sp.wait_ge(front_done, fronts_then)
                sp.dma_start(region, tab[bass.ds(first_row, PADDED), cols].rearrange("(n p) d -> p n d", p=P)).then_inc(a_loaded[c % 2], 16)

            def load_row(u, ap, width):
                if u >= 2:
                    sp.wait_ge(*row_free(u - 2))
                sp.dma_start(rows[0:ap.shape[0], u % 2, 0:width], ap).then_inc(rows_loaded[u % 2], 16)

            def source(v):
                name, half, _, _ = SOURCES[v]
                for n in range(TILES):
                    load_row(ROW_AT["source", v, n], rows_of[name][P * n:P * n + ROWS[n], HALF * half:HALF * (half + 1)], HALF)

            def epoch_end(e):
                last, how, to, rest, _, _ = EPOCHS[e]
                v = next(v for v in range(len(SOURCES)) if FIRST_USE[v] == last + 1)
                for j in range(TILES + 2):
                    if rest and j < TILES:
                        load_row(ROW_AT["rest", e, j], rows_of[rest][P * j:P * j + ROWS[j], :], FEATURES)
                    n = j - 1
                    if 0 <= n < TILES:
                        if how == "none":
                            sp.wait_ge(acc_done, GROUPS * last + 2 * (n + 1))
                        else:
                            sp.wait_ge(tail_done, TILES * TAILS[e] + n + 1)
                        sp.dma_start(rows_of[to][P * n:P * n + ROWS[n], :], acc[0:ROWS[n], n, :]).then_inc(stored[n % 2], 16)
                    n = j - 2
                    if 0 <= n:
                        sp.wait_ge(stored[n % 2], 16 * (5 * e + n // 2 + 1))
                        set_acc(e + 1, v, n)

            def set_acc(e, v, n):
                sp.wait_ge(t_ready, TILES * v + n + 1)
                b = bias[EPOCHS[e][4]].rearrange("(o f) -> o f", o=1)
                sp.dma_start(acc[0:ROWS[n], n, :], b.to_broadcast((ROWS[n], FEATURES))).then_inc(acc_set, 16)

            for n in range(TILES):
                set_acc(0, 0, n)
            s = 0
            while s < len(STEPS):
                graph, v, name, half = STEPS[s]
                g = G_BEFORE[s]
                if name == "rel":
                    with sp.Fori(0, RELATIONS) as r:
                        fronts_then = [sp.snap(FRONTS * (s + r) + o) for o in (2 * KT - FRONTS, 0, KT)]
                        first = sp.snap(r * PADDED)
                        load_weights(s + r, r * FEATURES + HALF * half, "rel")
                        for c, then in ((1, 0), (0, 1), (2, 2)):
                            load_counts(c, g + r, rtab2, first, fronts_then[then])
                    s += RELATIONS
                else:
                    if name != "edge":
                        load_weights(s, HALF * half, name)
                    if s == FIRST_GRAPH:
                        sp.wait_ge(zeroed["r"], 16 * ZERO_PIECES)
                    if graph:
                        sp.wait_ge(front_done, FRONTS * s - FRONTS + 2 * KT)
                        load_counts(1, g, atab2, 0)
                        sp.wait_ge(front_done, FRONTS * s)
                        load_counts(0, g, atab2, 0)
                    if FIRST_USE[v] == s:
                        if s - 1 in EPOCH_END:
                            epoch_end(EPOCH_END[s - 1])
                        if not SOURCES[v][2]:
                            source(v)
                    if name == "edge":
                        load_edge_weights(s)
                    if graph:
                        sp.wait_ge(front_done, FRONTS * s + KT)
                        load_counts(2, g, atab2, 0)
                    s += 1
            e = len(EPOCHS) - 1
            for j in range(TILES + 1):
                if j < TILES:
                    load_row(ROW_AT["rest", e, j], rows_of["x3"][P * j:P * j + ROWS[j], :], FEATURES)
                    if j >= 2:
                        sp.wait_ge(out_ready, j - 1)
                    else:
                        sp.wait_ge(w_lo_ready, KT * len(STEPS))
                    sp.dma_start(w_raw[0:ROWS[j], j % 2, :], rows_of["u"][P * j:P * j + ROWS[j], :]).then_inc(u_loaded[j % 2], 16)
                n = j - 1
                if n >= 0:
                    sp.wait_ge(out_ready, n + 1)
                    sp.dma_start(out[P * n:P * n + ROWS[n], :], acc[0:ROWS[n], n, :]).then_inc(stored[n % 2], 16)
            for i in range(2):
                sp.wait_ge(stored[i], 16 * 5 * len(EPOCHS))

        @block.gpsimd
        def _(pool):
            pool.memset(edges_i[:, :, :], 2000)
            pool.memset(edge_w[:, :], 0.0).then_inc(consts, 1)
            pool.memset(zeros[:, :], 0.0).then_inc(consts, 1)
            pool.memset(ones_f[:, :], 1.0).then_inc(consts, 1)
            pool.memset(eps[:, :], EPS).then_inc(consts, 1)
            pool.iota(spare_i[:, :], pattern=[[P, 4]], base=0, channel_multiplier=1).then_inc(consts, 1)
            pool.wait_ge(consts, 5)
            pool.affine_select(out=ident_f[:, :], in_=ones_f[:, :], compare_op=ALU.is_equal, fill=0.0, base=0,
                               pattern=[[-1, P]], channel_multiplier=1).then_inc(consts, 1)
            pool.affine_select(out=below[:, :], in_=ones_f[:, :], compare_op=ALU.is_gt, fill=0.0, base=0,
                               pattern=[[1, P]], channel_multiplier=-1).then_inc(consts, 1)
            for name, tabs in (("w", wtab), ("a", [atab]), ("r", [rtab])):
                for tab, link in zip(tabs, added[name]):
                    pool.dma_start(tab[tab.shape[0] - SPARE:].rearrange("(p c) o -> p (c o)", p=P), zeros[:, 0:4]).then_inc(link, 16)

            copied = 0
            for name, idx, val, tabs, ready in (("w", idx_w, wsum, wtab, 0), ("a", idx_a, cnt_a, [atab], 0),
                                                ("r", idx_r, cnt_r, [rtab], QUADS)):
                sems, T = added[name], len(tabs)
                zeros_of = 16 * (ZERO_PIECES if name == "r" else T)
                with pool.Fori(0, QUADS // 2) as i:
                    for b in range(2):
                        q = 2 * i + b
                        over = pool.snap(pool.to_reg(16 * (1 + 4 * (i if T > 1 else q))))
                        copies = pool.snap(pool.to_reg(q + 1 + copied))
                        pool.wait_ge(idx_ready, q + 3 + ready)
                        pool.wait_ge(sems[b % T], over)
                        pool.tensor_copy(idx_slot[:, b, :], idx[:, bass.ds(4 * q, 4)])
                        pool.tensor_copy(val_slot[:, b, :], val[:, bass.ds(4 * q, 4)]).then_inc(slot_ready, 1)
                        pool.wait_ge(zeroed[name], zeros_of)
                        pool.wait_ge(slot_ready, copies)
                        for j in range(4):
                            pool.indirect_dma_start(
                                out=tabs[b % T], out_offset=bass.IndirectOffsetOnAxis(ap=idx_slot[:, b, j:j + 1], axis=0),
                                in_=val_slot[:, b, j:j + 1], in_offset=None, compute_op=ALU.add).then_inc(sems[b % T], 16)
                for j in range(T):
                    pool.wait_ge(sems[j], 16 * (1 + EDGE_COLS // T))
                copied += QUADS

        @block.scalar
        def _(act):
            def pt_slot_free(s, c):
                value = GROUPS * s + (0, -GROUPS + 2 * CHUNKS[1][1], 2 * CHUNKS[0][1])[c]
                if not isinstance(value, int) or value > 0:
                    act.wait_ge(dense_done, value)

            def split_weights_hi(s, k):
                if isinstance(s, int) and s < 2:
                    act.wait_ge(in_added, WSUM * s + (TABLES - 1) * (k + 1))
                else:
                    act.wait_ge(raw_loaded[k], 16 * (s + 1))
                if not (isinstance(s, int) and s == 0):
                    act.wait_ge(dense_done, GROUPS * s)
                nc.scalar.activation(w_hi[:, k, :], w_raw[:, k, :], ACT.Copy).then_inc(w_hi_ready, 1)

            def fronts(s):
                for c in range(3):
                    for f in range(KT):
                        unit = KT * c + f
                        if f == 0:
                            pt_slot_free(s, c)
                        act.wait_ge(front_done, FRONTS * s + unit + 1)
                        nc.scalar.activation(pt_hi[c % 2][:, f, 0:WIDTH[c]], front_bank[unit % 3][:, 0:WIDTH[c]], ACT.Copy).then_inc(front_hi, 1)
                        if c == 0:
                            split_weights_hi(s, f)
                        if isinstance(s, int) and FRONTS * s + unit < ZERO_BY_ACT:
                            zero_piece(act, ZERO_PIECES - ZERO_BY_ACT + FRONTS * s + unit)

            def root_of_variance(m, n):
                act.wait_ge(moments_ready, TILES * m + n + 1)
                nc.scalar.activation(std[0:ROWS[n], n:n + 1], moments[0:ROWS[n], n, 1:2], ACT.Sqrt, bias=eps[0:ROWS[n], :]).then_inc(std_ready, 1)

            def source_tile(v, n, m=None, e=None):
                name, half, from_acc, norm = SOURCES[v]
                r, count = ROWS[n], TILES * v + n + 1
                if from_acc:
                    s_in = acc[0:r, n, 0:HALF]
                    if e == 1:
                        act.wait_ge(tail_done, TILES * TAILS[1] + n + 1)
                    if e == 4:
                        act.wait_ge(acc_done, GROUPS * EPOCHS[4][0] + 2 * (n + 1))
                else:
                    u = ROW_AT["source", v, n]
                    s_in = rows[0:r, u % 2, 0:HALF]
                    act.wait_ge(rows_loaded[u % 2], 16 * (u // 2 + 1))
                if count > 2:
                    act.wait_ge(h_ready, count - 2)
                if m is not None:
                    act.wait_ge(norm_ready, TILES * m + n + 1)
                t = t_buf[0:r, n % 2, :]
                if norm:
                    nc.scalar.activation(t, s_in, ACT.Relu, scale=scale[0:r, n:n + 1], bias=shift[0:r, n:n + 1]).then_inc(t_ready, 1)
                else:
                    nc.scalar.activation(t, s_in, ACT.Copy).then_inc(t_ready, 1)
                if v and n == 0:
                    act.wait_ge(front_done, FRONTS * (LAST_USE[v - 1] + 1))
                act.wait_ge(t_ready, count)
                nc.scalar.activation(h_hi[0:r, n, :], t, ACT.Copy).then_inc(h_hi_ready, 1)

            def sources_after(s):
                v = STEPS[s + 1][1]
                if FIRST_USE[v] != s + 1:
                    return
                e = EPOCH_END.get(s)
                boundary(v, e)

            def boundary(v, e):
                m = MOMENTS.get(e) if e is not None else None
                if m is not None:
                    for n in range(TILES):
                        root_of_variance(m, n)
                        if n:
                            source_tile(v, n - 1, m, e)
                    source_tile(v, TILES - 1, m, e)
                else:
                    for n in range(TILES):
                        source_tile(v, n, None, e)

            def spread(k, q, b):
                if not isinstance(q, int) or q + k:
                    act.wait_ge(cast_done, q + k * QUADS)
                act.wait_ge(keys_ready, 1)
                for j in range(4):
                    last = nc.scalar.activation(diag[:, b, j, :], ident_f[:, :], ACT.Copy, scale=key[k][:, bass.ds(4 * q + j, 1)])
                last.then_inc(diag_ready, 1)

            def copy_row(k, q, b):
                if not isinstance(q, int) or q + k:
                    act.wait_ge(same_ready, q + 1 + k * QUADS)
                act.wait_ge(cast_done, q + 2 + k * QUADS)
                nc.scalar.activation(key_row[:, b, :], cast_bank[b][:, :], ACT.Copy).then_inc(row_ready, 1)

            for k in range(2):
                spread(k, 0, 0)
                with act.Fori(0, QUADS // 2 - 1) as i:
                    for b in range(2):
                        spread(k, 2 * i + b + 1, 1 - b)
                        copy_row(k, 2 * i + b, b)
                spread(k, QUADS - 1, 1)
                copy_row(k, QUADS - 2, 0)
                copy_row(k, QUADS - 1, 1)
                if k == 0:
                    boundary(0, -1)
            s = 0
            while s < len(STEPS):
                if STEPS[s][2] == "rel":
                    with act.Fori(0, RELATIONS) as r:
                        fronts(s + r)
                    s += RELATIONS
                else:
                    fronts(s)
                    if s == FIRST_GRAPH:
                        act.wait_ge(self_degrees, 1)
                        nc.scalar.activation(deg_std[:, :], deg_std[:, :], ACT.Sqrt).then_inc(deg_root, 1)
                    s += 1
                if s < len(STEPS):
                    sources_after(s - 1)
            e = len(EPOCHS) - 1
            for n in range(TILES):
                r, u = ROWS[n], ROW_AT["rest", e, n]
                act.wait_ge(rows_loaded[u % 2], 16 * (u // 2 + 1))
                if n >= 2:
                    act.wait_ge(out_ready, n - 1)
                nc.scalar.activation(w_raw[0:r, 2 + n % 2, :], rows[0:r, u % 2, :], ACT.Relu, scale=scale[0:r, n:n + 1], bias=shift[0:r, n:n + 1])
                act.wait_ge(u_loaded[n % 2], 16 * (n // 2 + 1))
                nc.scalar.activation(w_raw[0:r, n % 2, :], w_raw[0:r, n % 2, :], ACT.Tanh).then_inc(gate_act, 1)

        @block.tensor
        def _(pe):
            def mm(o, l, r, start, stop, **kw):
                return nc.tensor.matmul(o, l, r, start=start, stop=stop, **kw)

            def cast(k, q, b):
                pe.wait_ge(diag_ready, q + 1 + k * QUADS)
                if not isinstance(q, int) or q + k:
                    pe.wait_ge(row_ready, q + k * QUADS)
                mm(cast_bank[b][:, :], ones_f[:, :], diag[:, b, :, :].rearrange("p j c -> p (j c)"), True, True).then_inc(cast_done, 1)

            def sum_equal(k, q, b):
                pe.wait_ge(same_ready, q + 3 + k * QUADS)
                if not isinstance(q, int) or q + k:
                    pe.wait_ge(idx_ready, q + 1 + k * QUADS)
                for c in range(4):
                    sums = stat_bank[b][:, 5 * c:5 * c + 5]
                    for j in range(4):
                        last = mm(sums, same[:, b, j, P * c:P * c + P],
                                  values[:, bass.ds(10 * (4 * q + j) + (5 if j < c else 0), 5)], j == 0, j == 3)
                        if j == 0:
                            mm(sums[:, 0:1], before[:, b, c, :], values[:, 1:2], False, False)
                last.then_inc(stat_done, 1)

            for k in range(2):
                cast(k, 0, 0)
                with pe.Fori(0, QUADS // 2 - 1) as i:
                    for b in range(2):
                        cast(k, 2 * i + b + 1, 1 - b)
                        sum_equal(k, 2 * i + b, b)
                cast(k, QUADS - 1, 1)
                sum_equal(k, QUADS - 2, 0)
                sum_equal(k, QUADS - 1, 1)

            def counts_loaded(c, g, with_self=False):
                if with_self:
                    pe.wait_ge(self_added, 3 * (g - FIRST_SELF) + c + 1)
                else:
                    pe.wait_ge(a_loaded[c % 2], 16 * (g + 1) if c == 1 else 16 * (2 * g + 1 + c // 2))

            def front(s, c, graph, v, g, with_self=False):
                a, b = CHUNKS[c]
                for f in range(KT):
                    unit = KT * c + f
                    cols = slice(P * f, P * f + P)
                    bank = front_bank[unit % 3]
                    if f == 0 and graph:
                        if c == 0:
                            pe.wait_ge(h_ready, TILES * (v + 1))
                        counts_loaded(c, g, with_self)
                    if not isinstance(s, int) or s or unit >= 3:
                        pe.wait_ge(front_lo, FRONTS * s + unit - 2)
                    if graph:
                        for n in range(TILES):
                            k = ROWS[n]
                            counts = a_chunk[c % 2][0:k, n, 0:WIDTH[c]]
                            mm(bank[:, 0:WIDTH[c]], h_hi[0:k, n, cols], counts, n == 0, False)
                            last = mm(bank[:, 0:WIDTH[c]], h_lo[0:k, n, cols], counts, False, n == TILES - 1)
                    else:
                        for n in range(a, b):
                            if f == 0:
                                pe.wait_ge(h_ready, TILES * v + n + 1)
                            k, first, second = ROWS[n], P * (n - a) // (2 * P) * 2 * P, (n - a) % 2
                            out, unit_of = bank[:, first:first + 2 * P], ident_wide[0:k, P * (1 - second):P * (3 - second)]
                            mm(out, h_hi[0:k, n, cols], unit_of, second == 0, False)
                            last = mm(out, h_lo[0:k, n, cols], unit_of, False, second == 1 or n == b - 1)
                    last.then_inc(front_done, 1)

            def degrees(t, c, g):
                counts_loaded(c, g)
                if not isinstance(t, int) or c:
                    pe.wait_ge(deg_used, 3 * t + c)
                for j in range(TILES):
                    k = ROWS[j]
                    last = mm(deg_bank[:, 0:WIDTH[c]], ones[0:k, :], a_chunk[c % 2][0:k, j, 0:WIDTH[c]], j == 0, j == TILES - 1)
                last.then_inc(deg_done, 1)

            def dense(s, c):
                if c == 0:
                    pe.wait_ge(w_lo_ready, KT * (s + 1))
                pe.wait_ge(front_lo, FRONTS * s + KT * (c + 1))
                for n in range(*CHUNKS[c]):
                    m, o = ROWS[n], P * (n - CHUNKS[c][0])
                    for half in range(2):
                        group = 2 * n + half
                        if not isinstance(s, int) or s or group >= 4:
                            pe.wait_ge(acc_done, GROUPS * s + group - 3)
                        bank = dense_bank[group % 4][0:m, :]
                        cols = slice(512 * half, 512 * half + 512)
                        for f in range(KT):
                            hi, lo = pt_hi[c % 2][:, f, o:o + m], pt_lo[c % 2][:, f, o:o + m]
                            mm(bank, hi, w_hi[:, f, cols], f == 0, False)
                            mm(bank, hi, w_lo[:, f, cols], False, False)
                            last = mm(bank, lo, w_hi[:, f, cols], False, f == KT - 1)
                        last.then_inc(dense_done, 1)

            def step(s, graph, v, g, table=None, with_self=False):
                for c in range(2):
                    if table is not None:
                        degrees(table, c, g)
                    front(s, c, graph, v, g, with_self)
                dense(s, 0)
                if table is not None:
                    degrees(table, 2, g)
                front(s, 2, graph, v, g, with_self)
                dense(s, 1)
                dense(s, 2)

            s = 0
            while s < len(STEPS):
                graph, v, name, half = STEPS[s]
                g = G_BEFORE[s]
                if name == "rel":
                    with pe.Fori(0, RELATIONS) as r:
                        step(s + r, graph, v, g + r, 1 + r if half == 0 else None)
                    s += RELATIONS
                    continue
                step(s, graph, v, g, 0 if s == FIRST_GRAPH else None, name == "gcn")
                s += 1

        @block.vector
        def _(dve):
            V = nc.vector
            count = [0]

            def link(ins):
                count[0] += 1
                ins.then_inc(small, 1)
                dve.wait_ge(small, count[0])

            dve.wait_ge(consts, 7)
            for i in (0, 2):
                V.tensor_scalar(ident_wide[:, P * i:P * i + P], ident_f[:, :], 0.0, None, ALU.mult)
            V.tensor_copy(ident[:, :], ident_f[:, :])
            V.tensor_copy(ones[:, :], ones_f[:, :]).then_inc(row_ready, 1)
            V.memset(deg_inv[:, :], 1.0).then_inc(cast_done, 1)
            V.memset(deg_std[:, :], 1.0).then_inc(same_ready, 2)
            V.memset(rel_inv[:, :], 1.0).then_inc(stat_done, 1)
            V.memset(std[:, :], 1.0).then_inc(idx_ready, 2)
            link(V.tensor_copy(spare["w"][:, :], spare_i[:, :]))
            V.tensor_scalar(spare["a"][:, :], spare["w"][:, :], float(NA), None, ALU.add)
            link(V.tensor_scalar(spare["r"][:, :], spare["w"][:, :], float(RELATIONS * NA), None, ALU.add))
            dve.wait_ge(edges_in, 64)
            link(V.tensor_copy(edges_f[:, :, :], edges_i[:, :, :]))
            link(V.tensor_scalar(spare["w"][:, :], spare["w"][:, :], float(NW), None, ALU.add))
            src_f, dst_f, type_f = (edges_f[:, i, :] for i in range(3))
            V.scalar_tensor_tensor(out=key_w[:, :], in0=dst_f, scalar=float(FEATURES), in1=src_f, op0=ALU.mult, op1=ALU.add)
            V.scalar_tensor_tensor(out=key[0][:, :], in0=src_f, scalar=float(NODES), in1=dst_f, op0=ALU.mult, op1=ALU.add)
            V.scalar_tensor_tensor(out=src_row[:, :], in0=type_f, scalar=float(PADDED), in1=src_f, op0=ALU.mult, op1=ALU.add)
            V.tensor_scalar(valid[:, 0, :], src_f, float(FEATURES), None, ALU.is_lt)
            link(V.tensor_scalar(valid[:, 1, :], src_f, float(NODES), None, ALU.is_lt))
            V.scalar_tensor_tensor(out=key[1][:, :], in0=src_row[:, :], scalar=float(NODES), in1=dst_f, op0=ALU.mult, op1=ALU.add)
            link(V.scalar_tensor_tensor(out=valid[:, 0, :], in0=dst_f, scalar=float(FEATURES), in1=valid[:, 0, :], op0=ALU.is_lt, op1=ALU.mult))

            def quads(ap):
                return ap.rearrange("p (q j) -> p q j", j=4)

            rows_and_masks = (("w", key_w, 0), ("a", key[0], 1), ("r", key[1], 1))
            for name, k, ok in rows_and_masks:
                last = V.tensor_tensor(quads(off[name][:, :]), quads(k[:, :]), spare[name][:, :].unsqueeze(1).to_broadcast((P, QUADS, 4)), ALU.subtract)
            link(last)
            for name, k, ok in rows_and_masks:
                V.tensor_tensor(off[name][:, :], off[name][:, :], valid[:, ok, :], ALU.mult)
            link(V.tensor_copy(part[:, 0, :], edge_w[:, :]))
            link(V.tensor_tensor(edge_w[:, :], edge_w[:, :], part[:, 0, :], ALU.subtract))
            link(V.tensor_copy(part[:, 1, :], edge_w[:, :]))
            link(V.tensor_tensor(part[:, 2, :], edge_w[:, :], part[:, 1, :], ALU.subtract))
            by_edge = values[:, :].rearrange("p (t a c) -> p t a c", a=2, c=5)
            for a in range(2):
                V.memset(by_edge[:, :, a, 0:1], float(a))
                V.memset(by_edge[:, :, a, 1:2], 1.0)
                last = V.tensor_copy(by_edge[:, :, a, 2:5], part[:, :, :].rearrange("p c t -> p t c"))
            last.then_inc(keys_ready, 1)
            dve.wait_ge(keys_ready, 1)

            def compare(k):
                names = "wa" if k == 0 else "r"

                def mark(q, b):
                    dve.wait_ge(row_ready, q + 2 + k * QUADS)
                    if not isinstance(q, int) or q + k:
                        dve.wait_ge(stat_done, q + k * QUADS)
                    for j in range(4):
                        last = V.tensor_scalar(same[:, b, j, :], key_row[:, b, :], key[k][:, bass.ds(4 * q + j, 1)], None, ALU.is_equal)
                    last.then_inc(equal_done, 1)
                    dve.wait_ge(equal_done, q + 1 + k * QUADS)
                    for j in range(4):
                        last = V.tensor_tensor(before[:, b, j, :], same[:, b, j, P * j:P * j + P], below[:, :], ALU.mult)
                    last.then_inc(same_ready, 1)

                def take_sums(q, b):
                    cols = bass.ds(4 * q, 4)
                    dve.wait_ge(stat_done, q + 2 + k * QUADS)
                    sums = stat_bank[b][:, 0:20].rearrange("p (j c) -> p j c", c=5)
                    for m, name in enumerate(names):
                        last = V.scalar_tensor_tensor(out=idx_f[:, b, m, :], in0=sums[:, :, 0], scalar=0.5, in1=off[name][:, cols],
                                                      op0=ALU.is_lt, op1=ALU.mult)
                    last.then_inc(row_done, 1)
                    if k == 0:
                        V.tensor_reduce(wsum[:, cols], sums[:, :, 2:5], mybir.AxisListType.X, ALU.add)
                    V.tensor_copy((cnt_a if k == 0 else cnt_r)[:, cols], sums[:, :, 1])
                    dve.wait_ge(row_done, q + 1 + k * QUADS)
                    for m, name in enumerate(names):
                        last = V.tensor_tensor({"w": idx_w, "a": idx_a, "r": idx_r}[name][:, cols], idx_f[:, b, m, :],
                                               spare[name][:, :], ALU.add)
                    last.then_inc(idx_ready, 1)

                mark(0, 0)
                with dve.Fori(0, QUADS // 2 - 1) as i:
                    for b in range(2):
                        mark(2 * i + b + 1, 1 - b)
                        take_sums(2 * i + b, b)
                mark(QUADS - 1, 1)
                take_sums(QUADS - 2, 0)
                take_sums(QUADS - 1, 1)

            def take_moments(m, n):
                r = ROWS[n]
                if TILES * m + n >= 2:
                    dve.wait_ge(moments_ready, TILES * m + n - 1)
                for i in range(2):
                    last = V.bn_stats(partial[0:r, n % 2, i, :], acc[0:r, n, HALF * i:HALF * (i + 1)])
                link(last)
                V.bn_aggr(moments[0:r, n, :], partial[0:r, n % 2, :, :].rearrange("p a b -> p (a b)")).then_inc(moments_ready, 1)

            def take_norm(m, n, e):
                r, c = ROWS[n], slice(n, n + 1)
                dve.wait_ge(std_ready, TILES * m + n + 1)
                link(V.reciprocal(scale[0:r, c], std[0:r, c]))
                if e == 2:
                    link(V.tensor_tensor(scale[0:r, c], scale[0:r, c], dinv[0:r, c], ALU.mult))
                V.scalar_tensor_tensor(out=shift[0:r, c], in0=moments[0:r, n, 0:1], scalar=-1.0, in1=scale[0:r, c],
                                       op0=ALU.mult, op1=ALU.mult).then_inc(norm_ready, 1)

            def source_lo(v, n):
                r = ROWS[n]
                dve.wait_ge(h_hi_ready, TILES * v + n + 1)
                V.tensor_tensor(h_lo[0:r, n, :], t_buf[0:r, n % 2, :], h_hi[0:r, n, :].bitcast(FP32), ALU.subtract).then_inc(h_ready, 1)

            def tail(e, n):
                last, how, _, _, _, _ = EPOCHS[e]
                r = ROWS[n]
                dve.wait_ge(acc_done, GROUPS * last + 2 * (n + 1))
                if how == "relu":
                    V.tensor_scalar(acc[0:r, n, :], acc[0:r, n, :], 0.0, None, ALU.max).then_inc(tail_done, 1)
                    return
                u = ROW_AT["rest", e, n]
                dve.wait_ge(rows_loaded[u % 2], 16 * (u // 2 + 1))
                rest = rows[0:r, u % 2, :]
                if how == "add":
                    V.tensor_tensor(acc[0:r, n, :], acc[0:r, n, :], rest, ALU.add).then_inc(tail_done, 1)
                else:
                    V.scalar_tensor_tensor(out=acc[0:r, n, :], in0=acc[0:r, n, :], scalar=0.0, in1=rest, op0=ALU.max, op1=ALU.add).then_inc(tail_done, 1)
                dve.wait_ge(tail_done, TILES * TAILS[e] + n + 1)

            def final(n):
                r, u = ROWS[n], ROW_AT["rest", len(EPOCHS) - 1, n]
                th, h3, x3, z = w_raw[0:r, n % 2, :], w_raw[0:r, 2 + n % 2, :], rows[0:r, u % 2, :], acc[0:r, n, :]
                dve.wait_ge(gate_act, n + 1)
                link(V.tensor_tensor(th, th, h3, ALU.subtract))
                dve.wait_ge(acc_done, GROUPS * LAST + 2 * (n + 1))
                V.tensor_tensor(h3, h3, x3, ALU.add)
                link(V.tensor_tensor(th, th, z, ALU.mult))
                V.tensor_tensor(z, th, h3, ALU.add).then_inc(out_ready, 1)

            def after_step(s):
                jobs = [[] for _ in range(13)]
                if s == LAST:
                    for n in range(TILES):
                        jobs[n if n < 8 else 2 * n - 7].append(lambda n=n: final(n))
                    return jobs
                v = STEPS[s + 1][1]
                if FIRST_USE[v] != s + 1:
                    return jobs
                e = EPOCH_END.get(s)
                for n in range(TILES):
                    slot = n if n < 8 or e is None else 2 * n - 7
                    if e is None:
                        jobs[slot].append(lambda n=n: source_lo(v, n))
                        continue
                    if EPOCHS[e][1] != "none":
                        jobs[slot].append(lambda n=n: tail(e, n))
                    if EPOCHS[e][5]:
                        m = MOMENTS[e]
                        jobs[slot].append(lambda n=n: take_moments(m, n))
                        if n:
                            jobs[slot].append(lambda n=n: take_norm(m, n - 1, e))
                        if n > 1:
                            jobs[slot].append(lambda n=n: source_lo(v, n - 2))
                    elif n:
                        jobs[slot].append(lambda n=n: source_lo(v, n - 1))
                if e is not None:
                    if EPOCHS[e][5]:
                        jobs[12] += [lambda: take_norm(MOMENTS[e], TILES - 1, e), lambda: source_lo(v, TILES - 2)]
                    jobs[12].append(lambda: source_lo(v, TILES - 1))
                return jobs

            def add_edge_weights(s):
                for k in range(KT):
                    for j in range(TABLES - 1):
                        q = WSUM * s + (TABLES - 1) * k + j
                        dve.wait_ge(in_loaded[q % WSUM], 16 * (q // WSUM + 1))
                        dve.wait_ge(raw_loaded[k], 16 * (s + 1))
                        if j:
                            dve.wait_ge(in_added, q)
                        V.tensor_tensor(w_raw[:, k, :], w_raw[:, k, :], in_buf[:, q % WSUM, :], ALU.add).then_inc(in_added, 1)

            def add_self_loops(g, c):
                a, b = CHUNKS[c]
                dve.wait_ge(a_loaded[c % 2], 16 * (g + 1) if c == 1 else 16 * (2 * g + 1 + c // 2))
                for n in range(a, b):
                    w = ROWS[n]
                    block_n = a_chunk[c % 2][0:w, n, P * (n - a):P * (n - a) + w]
                    last = V.tensor_tensor(block_n, block_n.bitcast(FP32), ident[0:w, 0:w].bitcast(FP32), ALU.add)
                last.then_inc(self_added, 1)

            def take_degrees(t, c, at_least, inverted):
                dve.wait_ge(deg_done, 3 * t + c + 1)
                a, b = CHUNKS[c]
                blocks = t_buf[:, 0, 0:P * (b - a)].rearrange("p (n d) -> p n d", d=P)
                for n in range(a, b):
                    m, o = ROWS[n], P * (n - a)
                    last = V.tensor_tensor(blocks[:, n - a, 0:m], deg_bank[:, o:o + m], ident[:, 0:m].bitcast(FP32), ALU.mult)
                last.then_inc(deg_used, 1)
                dve.wait_ge(deg_used, 3 * t + c + 1)
                whole = min(b, TILES - 1)
                last = V.tensor_reduce(deg_std[:, a:whole], blocks[:, 0:whole - a, :], mybir.AxisListType.X, ALU.add)
                if b == TILES:
                    last = V.tensor_reduce(deg_std[:, b - 1:b], blocks[:, b - 1 - a, 0:ROWS[-1]], mybir.AxisListType.X, ALU.add)
                steps = 3 * (3 * t + c) + 1
                last.then_inc(deg_small, 1)
                dve.wait_ge(deg_small, steps)
                V.tensor_scalar(at_least, deg_std[:, a:b], 1.0, None, ALU.max).then_inc(deg_small, 1)
                dve.wait_ge(deg_small, steps + 1)
                V.reciprocal(inverted, at_least).then_inc(deg_small, 1)
                dve.wait_ge(deg_small, steps + 2)

            def step(s, graph, name, half, r=None, jobs=None):
                def low_part(unit):
                    c, f = divmod(unit, KT)
                    dve.wait_ge(front_hi, FRONTS * s + unit + 1)
                    V.tensor_tensor(pt_lo[c % 2][:, f, 0:WIDTH[c]], front_bank[unit % 3][:, 0:WIDTH[c]],
                                    pt_hi[c % 2][:, f, 0:WIDTH[c]].bitcast(FP32), ALU.subtract).then_inc(front_lo, 1)

                def add_group(group):
                    n, o = divmod(group, 2)
                    m = ROWS[n]
                    dve.wait_ge(dense_done, GROUPS * s + group + 1)
                    tile = acc[0:m, n, 512 * o:512 * o + 512]
                    bank = dense_bank[group % 4][0:m, :]
                    if graph:
                        by = rel_inv[0:m, bass.ds(TILES * r + n, 1)] if r is not None else (dinv if name == "gcn" else deg_inv)[0:m, n:n + 1]
                        V.scalar_tensor_tensor(out=tile, in0=bank, scalar=by, in1=tile, op0=ALU.mult, op1=ALU.add).then_inc(acc_done, 1)
                    else:
                        V.tensor_tensor(tile, bank, tile, ALU.add).then_inc(acc_done, 1)

                if name == "edge":
                    add_edge_weights(s)
                def chunk_degrees(c):
                    a, b = CHUNKS[c]
                    if r is not None and half == 0:
                        take_degrees(1 + r, c, deg_std[:, a:b], rel_inv[:, bass.ds(TILES * r + a, b - a)])
                    elif isinstance(s, int) and s == FIRST_GRAPH:
                        take_degrees(0, c, deg_inv[:, a:b], deg_inv[:, a:b])

                chunk_degrees(0)
                if name == "gcn":
                    add_self_loops(G_BEFORE[s], 0)
                    add_self_loops(G_BEFORE[s], 1)
                for f in range(KT):
                    low_part(f)
                    dve.wait_ge(w_hi_ready, KT * s + f + 1)
                    V.tensor_tensor(w_lo[:, f, :], w_raw[:, f, :], w_hi[:, f, :].bitcast(FP32), ALU.subtract).then_inc(w_lo_ready, 1)
                chunk_degrees(1)
                for f in range(KT):
                    low_part(KT + f)
                if isinstance(s, int) and (s == 0 or s - 1 in EPOCH_END):
                    epoch = 0 if s == 0 else EPOCH_END[s - 1] + 1
                    dve.wait_ge(acc_set, 16 * TILES * (epoch + 1))
                for group in range(2 * CHUNKS[0][1]):
                    if name == "gcn" and group == 6:
                        add_self_loops(G_BEFORE[s], 2)
                    add_group(group)
                chunk_degrees(2)
                if isinstance(s, int) and s == FIRST_GRAPH:
                    V.tensor_scalar(deg_std[:, :], deg_std[:, :], 1.0, None, ALU.add).then_inc(self_degrees, 1)
                for f in range(KT):
                    low_part(2 * KT + f)
                for slot, group in enumerate(range(2 * CHUNKS[0][1], GROUPS)):
                    add_group(group)
                    for job in (jobs[slot] if jobs else ()):
                        job()
                for job in (jobs[12] if jobs else ()):
                    job()

            compare(0)
            dve.wait_ge(x_in, 32)
            for n in range(TILES):
                take_moments(0, n)
                if n:
                    take_norm(0, n - 1, -1)
                if n > 1:
                    source_lo(0, n - 2)
            take_norm(0, TILES - 1, -1)
            source_lo(0, TILES - 2)
            source_lo(0, TILES - 1)
            compare(1)
            s = 0
            while s < len(STEPS):
                graph, v, name, half = STEPS[s]
                if name == "rel":
                    with dve.Fori(0, RELATIONS - 1) as r:
                        step(s + r, graph, name, half, r)
                    s += RELATIONS
                    step(s - 1, graph, name, half, RELATIONS - 1, after_step(s - 1))
                    continue
                step(s, graph, name, half, None, after_step(s))
                if s == FIRST_GRAPH:
                    dve.wait_ge(deg_root, 1)
                    link(V.reciprocal(dinv[:, :], deg_std[:, :]))
                s += 1


_INPUTS = ["x", "src", "dst", "edge_type_8", "edge_weight", "L0_gnn_bias", "L1_gnn_W_self0", "L1_gnn_W_neigh0", "L1_gnn_b0",
           "L1_gnn_W_self1", "L1_gnn_W_neigh1", "L1_gnn_b1", "L2_gnn_W", "L2_gnn_b", "L3_gnn_weight", "L3_gnn_root",
           "L3_gnn_bias", "L3_gnn_w_gate", "L3_gnn_b_gate"]


def kernel(**inputs):
    import numpy as _np
    import concourse.bacc as _bacc
    from concourse import mybir as _mybir
    from concourse.bass_utils import run_bass_kernel_spmd as _run

    nc = _bacc.Bacc("TRN2", target_bir_lowering=False, num_devices=1)
    arrays, args = {}, []
    for name in _INPUTS:
        a = _np.ascontiguousarray(inputs[name])
        arrays[f"in_{name}"] = a
        args.append(nc.dram_tensor(f"in_{name}", a.shape, _mybir.dt.from_np(a.dtype), kind="ExternalInput").ap())
    out = nc.dram_tensor("out_0", (NODES, FEATURES), FP32, kind="ExternalOutput").ap()
    build(nc, *args, out)
    r = _run(nc, [arrays], core_ids=[0])
    return r.results[0]["out_0"]
```

```python
import concourse.bass as bass
from concourse import mybir
from contextlib import ExitStack

FP32 = mybir.dt.float32
F32R = mybir.dt.float32r
BF16 = mybir.dt.bfloat16
I32 = mybir.dt.int32
ALU = mybir.AluOpType
ACT = mybir.ActivationFunctionType

P = 128
NODES = 1250
FEATURES = 1024
EDGES = 20000
RELATIONS = 8
HALF = FEATURES // 2
KT = HALF // P
TILES = -(-NODES // P)
ROWS = [min(P, NODES - P * n) for n in range(TILES)]
PADDED = TILES * P
CHUNKS = [(0, 4), (4, 7), (7, 10)]
WIDTH = [sum(ROWS[a:b]) for a, b in CHUNKS]
START = [P * a for a, _ in CHUNKS]
GROUPS = 2 * TILES
FRONTS = KT * len(CHUNKS)
EDGE_ROWS = 125
EDGE_COLS = EDGES // EDGE_ROWS
QUADS = EDGE_COLS // 4
TABLES = 2
SPARE = 4 * P
ZERO_PIECES = 10 * RELATIONS
COLS = 2 * RELATIONS + 3
BATCH = 8
BATCHES = EDGE_COLS // BATCH
BATCH_AT = {sg: i for i, sg in enumerate([(2, g) for g in range(1, 13)] + [(3, g) for g in range(BATCHES - 12)])}
NW = FEATURES * FEATURES
NA = PADDED * NODES
EPS = 1e-5

SOURCES = [("x", 0, True, True), ("x", 1, False, True),
           ("x1", 0, True, True), ("x1", 1, False, True), ("x1", 0, False, True),
           ("g", 0, True, False), ("g", 1, False, False),
           ("x2", 0, True, True), ("x2", 1, False, True),
           ("x3", 0, True, True), ("x3", 1, False, True),
           ("u", 0, True, False), ("u", 1, False, False),
           ("x3", 0, False, True), ("x3", 1, False, True)]
STEPS = [(False, 0, "edge", 0), (False, 1, "edge", 1),
         (False, 2, "self0", 0), (False, 3, "self0", 1), (True, 3, "neigh0", 1), (True, 4, "neigh0", 0),
         (False, 5, "self1", 0), (True, 5, "neigh1", 0), (False, 6, "self1", 1), (True, 6, "neigh1", 1),
         (True, 7, "gcn", 0), (True, 8, "gcn", 1),
         (False, 9, "root", 0)] + [(True, 9, "rel", 0)] * RELATIONS + [
         (False, 10, "root", 1)] + [(True, 10, "rel", 1)] * RELATIONS + [
         (False, 11, "gate", 0), (False, 12, "gate", 1), (False, 13, "gate", 2), (False, 14, "gate", 3)]
G_BEFORE = [sum(t[0] for t in STEPS[:s]) for s in range(len(STEPS))]
LAST = len(STEPS) - 1
FIRST_SELF = G_BEFORE[[t[2] for t in STEPS].index("gcn")]
EPOCHS = [(1, "add", "x1", "x", "b0", True), (5, "relu", "g", None, "b10", False),
          (9, "add", "x2", "x1", "b11", True), (11, "relu_add", "x3", "x2", "b2", True),
          (29, "none", "u", None, "b3", False), (LAST, "gate", "out", "x3", "bg", False)]
EPOCH_END = {e[0]: n for n, e in enumerate(EPOCHS)}
LAST_USE = [max(s for s, t in enumerate(STEPS) if t[1] == v) for v in range(len(SOURCES))]
FIRST_USE = [min(s for s, t in enumerate(STEPS) if t[1] == v) for v in range(len(SOURCES))]
FIRST_GRAPH = min(s for s, t in enumerate(STEPS) if t[0])
MOMENTS = {-1: 0, 0: 1, 2: 2, 3: 3}
EARLY = 3
TAILS = {1: 0, 3: 1}
ADDS = {0: 0, 2: 1}

WSUM = KT * (TABLES - 1)
ZERO_FROM = 2
ROW_USES = []
for _v, (_, _, _from_acc, _) in enumerate(SOURCES):
    for _e, _ep in enumerate(EPOCHS[:-1]):
        if FIRST_USE[_v] == _ep[0] + 1 and _ep[1] == "relu_add":
            ROW_USES += [("rest", _e, n) for n in range(TILES)]
    if not _from_acc:
        ROW_USES += [("source", _v, n) for n in range(TILES)]
    for _e, _ep in enumerate(EPOCHS):
        if _ep[1] == "add" and FIRST_USE[_v] == (EPOCHS[_e - 1][0] + 1 if _e else 0):
            ROW_USES += [("bias", _e, 0)]
ROW_USES += [("rest", len(EPOCHS) - 1, n) for n in range(TILES)]
ROW_AT = {u: i for i, u in enumerate(ROW_USES)}


def build(nc, x, src, dst, etype, eweight, b0, self0, neigh0, b10, self1, neigh1, b11, gcn, b2, rel,
          root, b3, gate, bg, out):
    def dram(name, shape):
        return nc.dram_tensor(name, shape, FP32, kind="Internal").ap()

    wtab = [dram(f"wtab{j}", (NW + SPARE, 1)) for j in range(TABLES)]
    atab = dram("atab", (NA + SPARE, 1))
    rtab = dram("rtab", (RELATIONS * NA + SPARE, 1))
    rows_of = {"x": x, "out": out}
    for name in ("x1", "x2", "x3", "g", "u"):
        rows_of[name] = dram(name, (NODES, FEATURES))
    weights = {"self0": self0, "neigh0": neigh0, "self1": self1, "neigh1": neigh1, "gcn": gcn,
               "root": root, "gate": gate, "rel": rel.rearrange("r k o -> (r k) o")}
    bias = {"b0": b0, "b10": b10, "b11": b11, "b2": b2, "b3": b3, "bg": bg}
    wtab2 = [t[0:NW].rearrange("(d s) c -> d (s c)", s=FEATURES) for t in wtab]
    atab2 = atab[0:NA].rearrange("(s d) c -> s (d c)", d=NODES)
    rtab2 = rtab[0:RELATIONS * NA].rearrange("(s d) c -> s (d c)", d=NODES)

    ctx = ExitStack()
    with ctx:
        base = nc.sbuf_base
        arena = ctx.enter_context(nc.sbuf_tensor("arena", [P, 212768], mybir.dt.uint8))
        top = [-(-base // 32) * 32]

        def place(name, shape, dt, at=None):
            size = 2 if dt == BF16 else 4
            for d in shape[1:]:
                size *= d
            if at is None:
                at = top[0]
                top[0] = -(-(at + size) // 32) * 32
                assert top[0] <= base + 212768, (name, top[0] - base)
            return nc.alloc_sbuf_tensor_at(name, shape, dt, offset=at)

        def sem(name):
            return ctx.enter_context(nc.semaphore(name))

        h_hi = place("h_hi", [P, TILES, HALF], F32R)
        h_lo = place("h_lo", [P, TILES, HALF], F32R)
        pt_hi_at = top[0]
        pt_hi = [place(f"pt_hi{i}", [P, KT, WIDTH[i]], F32R) for i in range(2)]
        pt_lo = [place(f"pt_lo{i}", [P, KT, WIDTH[i]], F32R) for i in range(2)]
        w_raw_at = top[0]
        w_raw = place("w_raw", [P, KT, FEATURES], FP32)
        w_hi = place("w_hi", [P, KT, FEATURES], F32R)
        w_lo = place("w_lo", [P, KT, FEATURES], F32R)
        acc = place("acc", [P, TILES, FEATURES], FP32)
        counts_at = top[0]
        a_chunk = [place(f"a_chunk{i}", [P, TILES, WIDTH[i]], F32R) for i in range(2)]
        rows = place("rows", [P, 2, FEATURES], FP32)
        t_buf = place("t_buf", [P, 2, HALF], FP32)
        ident_wide = place("ident_wide", [P, 3 * P], F32R)
        ident = ident_wide[:, P:2 * P]
        idx_r = place("idx_r", [P, EDGE_COLS], I32)
        cnt_r = place("cnt_r", [P, EDGE_COLS], FP32)
        idx_slot = place("idx_slot", [P, 2, 4], I32)
        val_slot = place("val_slot", [P, 2, 4], FP32)
        moments = place("moments", [P, TILES, 2], FP32)
        partial = place("partial", [P, 2, 2, 6], FP32)
        std = place("std", [P, TILES], FP32)
        scale = place("scale", [P, TILES], FP32)
        shift = place("shift", [P, TILES], FP32)
        deg_inv = place("deg_inv", [P, TILES], FP32)
        deg_std = place("deg_std", [P, TILES], FP32)
        dinv = place("dinv", [P, TILES], FP32)
        rel_inv = place("rel_inv", [P, RELATIONS * TILES], FP32)
        eps = place("eps", [P, 1], FP32)
        few_zeros = place("few_zeros", [P, NODES // 5], FP32)
        in_buf = place("in_buf", [P, WSUM, FEATURES], FP32, counts_at)
        late_at = counts_at + 27200
        at = [counts_at]

        def prep(name, shape, dt):
            size = 2 if dt == BF16 else 4
            for d in shape[1:]:
                size *= d
            t = place(name, shape, dt, at[0])
            at[0] += -(-size // 32) * 32
            return t

        same = prep("same", [P, 2, 4, 4 * P], BF16)
        before = prep("before", [P, 2, 4, P], BF16)
        ident_f = prep("ident_f", [P, P], FP32)
        ones_f = prep("ones_f", [P, P], FP32)
        below = prep("below", [P, P], BF16)
        idx_w = prep("idx_w", [P, EDGE_COLS], I32)
        wsum = prep("wsum", [P, EDGE_COLS], FP32)
        key = prep("key", [P, EDGE_COLS], FP32)
        off = {name: prep(f"off_{name}", [P, EDGE_COLS], FP32) for name in "war"}
        tot = prep("tot", [P, 2, 4, 2], FP32)
        own = prep("own", [P, 2, 4, 2], FP32)
        by_type = prep("by_type", [P, 2, 4, 2 * RELATIONS], FP32)
        spare_i = prep("spare_i", [P, 4], I32)
        spare = {name: prep(f"spare_{name}", [P, 4], FP32) for name in "war"}
        idx_f = prep("idx_f", [P, 2, 3, 4], FP32)
        assert at[0] <= counts_at + WSUM * FEATURES * 4, at[0] - counts_at
        at[0] = late_at
        diag = place("diag", [P, 2, 4, P], FP32, pt_hi_at)
        key_row = place("key_row", [P, 2, 4 * P], FP32, pt_hi_at + 2 * 4 * P * 4)
        values = place("values", [P, EDGE_COLS * 2 * COLS], BF16, w_raw_at)
        at_late, at[0] = at[0], counts_at + WSUM * FEATURES * 4
        iota_i = prep("iota_i", [P, P], I32)
        iota = prep("iota", [P, P], FP32)
        lo_i = prep("lo_i", [P, EDGE_COLS], I32)
        dst_lo = prep("dst_lo", [P, EDGE_COLS], FP32)
        dst_tile = prep("dst_tile", [P, EDGE_COLS], FP32)
        hot_lo = prep("hot_lo", [P, 2, BATCH, P], BF16)
        hot_tile = prep("hot_tile", [P, 2, BATCH, RELATIONS * TILES], BF16)
        assert at[0] <= late_at
        at[0] = at_late
        idx_a = prep("idx_a", [P, EDGE_COLS], I32)
        cnt_a = prep("cnt_a", [P, EDGE_COLS], FP32)
        zeros = prep("zeros", [P, NODES], FP32)
        assert at[0] <= counts_at + TILES * (WIDTH[0] + WIDTH[1]) * 4
        at[0] = -(-(base) // 32) * 32
        edges_i = prep("edges_i", [P, 3, EDGE_COLS], I32)
        edges_f = prep("edges_f", [P, 3, EDGE_COLS], FP32)
        edge_w = prep("edge_w", [P, EDGE_COLS], FP32)
        part = prep("part", [P, 3, EDGE_COLS], BF16)
        valid = prep("valid", [P, 2, EDGE_COLS], FP32)
        src_row = prep("src_row", [P, EDGE_COLS], FP32)
        key_w = prep("key_w", [P, EDGE_COLS], FP32)
        key_r = prep("key_r", [P, EDGE_COLS], FP32)

        banks = [ctx.enter_context(nc.psum_tensor(f"bank{i}", [P, 512], FP32)) for i in range(8)]
        front_bank, dense_bank, deg_bank = banks[0:3], banks[3:7], banks[7]
        cast_bank, stat_bank = banks[3:5], banks[5:7]

        edges_in = sem("edges_in")
        x_in = sem("x_in")
        consts = sem("consts")
        small = sem("small")
        keys_ready = sem("keys_ready")
        equal_done = sem("equal_done")
        sum_step = sem("sum_step")
        row_done = sem("row_done")
        zeroed = {name: sem(f"zeroed_{name}") for name in "war"}
        diag_ready = sem("diag_ready")
        cast_done = sem("cast_done")
        row_ready = sem("row_ready")
        same_ready = sem("same_ready")
        stat_done = sem("stat_done")
        idx_ready = sem("idx_ready")
        slot_ready = sem("slot_ready")
        added = {"w": [sem(f"added_w{j}") for j in range(TABLES)],
                 "a": [sem("added_a")], "r": [sem("added_r")]}
        in_loaded = [sem(f"in_loaded{i}") for i in range(WSUM)]
        in_added = sem("in_added")
        self_added = sem("self_added")
        raw_loaded = [sem(f"raw_loaded{k}") for k in range(KT)]
        w_hi_ready = sem("w_hi_ready")
        w_lo_ready = sem("w_lo_ready")
        a_loaded = [sem(f"a_loaded{i}") for i in range(2)]
        front_done = sem("front_done")
        front_hi = sem("front_hi")
        front_lo = sem("front_lo")
        dense_done = sem("dense_done")
        acc_done = sem("acc_done")
        hot_ready = sem("hot_ready")
        hot_used = sem("hot_used")
        degrees_ready = sem("degrees_ready")
        deg_root = sem("deg_root")
        moments_ready = sem("moments_ready")
        std_ready = sem("std_ready")
        norm_ready = sem("norm_ready")
        tail_done = sem("tail_done")
        rows_loaded = [sem(f"rows_loaded{i}") for i in range(2)]
        u_loaded = [sem(f"u_loaded{i}") for i in range(2)]
        t_ready = sem("t_ready")
        h_hi_ready = sem("h_hi_ready")
        h_ready = sem("h_ready")
        stored = [sem(f"stored{i}") for i in range(4)]
        acc_set = sem("acc_set")
        bias_added = sem("bias_added")
        gate_act = sem("gate_act")
        out_ready = sem("out_ready")

        block = ctx.enter_context(nc.Block())

        def row_free(use):
            kind, which, n = ROW_USES[use]
            if kind == "source":
                return t_ready, TILES * which + n + 1
            if kind == "bias":
                return bias_added, TILES * (ADDS[which] + 1)
            if which == len(EPOCHS) - 1:
                return out_ready, n + 1
            return tail_done, TILES * TAILS[which] + n + 1

        def zero_piece(eng, i):
            piece = rtab[i * P * NODES:(i + 1) * P * NODES].rearrange("(p c w) o -> p c (w o)", p=P, c=5)
            eng.dma_start(piece, few_zeros[:, None, :].to_broadcast((P, 5, NODES // 5))).then_inc(zeroed["r"], 16)

        @block.sync
        def _(sp):
            sp.wait_ge(consts, 1)
            for i, a in enumerate((src, dst, etype)):
                sp.dma_start(edges_i[0:EDGE_ROWS, i, :], a.rearrange("(p t) -> p t", p=EDGE_ROWS)).then_inc(edges_in, 16)
            sp.dma_start(edge_w[0:EDGE_ROWS, :], eweight.rearrange("(p t) -> p t", p=EDGE_ROWS)).then_inc(edges_in, 16)
            sp.wait_ge(consts, 2)
            for name, tabs, n, width in (("w", wtab, NW, FEATURES), ("a", [atab], NA, NODES)):
                for tab in tabs:
                    piece = tab[0:n].rearrange("(p c w) o -> p c (w o)", p=P, w=width)
                    sp.dma_start(piece, zeros[:, None, 0:width].to_broadcast((P, piece.shape[1], width))).then_inc(zeroed[name], 16)
                if name == "w":
                    full = TILES - 1
                    sp.dma_start(acc[:, 0:full, :], x[0:full * P, :].rearrange("(n p) f -> p n f", p=P)).then_inc(x_in, 16)
                    sp.dma_start(acc[0:ROWS[full], full, :], x[full * P:, :]).then_inc(x_in, 16)
            def load_weights(s, first_row, name):
                for k in range(KT):
                    if k == 0 and not (isinstance(s, int) and s == 0):
                        sp.wait_ge(w_lo_ready, KT * s)
                    sp.dma_start(w_raw[:, k, :], weights[name][bass.ds(first_row + P * k, P), :]).then_inc(raw_loaded[k], 16)

            def load_in(q, src_ap):
                if q >= WSUM:
                    sp.wait_ge(in_added, q - WSUM + 1)
                sp.dma_start(in_buf[:, q % WSUM, :], src_ap).then_inc(in_loaded[q % WSUM], 16)

            def load_edge_weights(s):
                if s == 0:
                    sp.wait_ge(idx_ready, 2 + QUADS)
                    for j in range(TABLES):
                        sp.wait_ge(added["w"][j], 16 * (1 + 2 * QUADS))
                for k in range(KT):
                    d = HALF * s + P * k
                    if s and k == 0:
                        sp.wait_ge(w_lo_ready, KT * s)
                    sp.dma_start(w_raw[:, k, :], wtab2[0][d:d + P, :]).then_inc(raw_loaded[k], 16)
                    for j in range(1, TABLES):
                        load_in(WSUM * s + (TABLES - 1) * k + j - 1, wtab2[j][d:d + P, :])

            def load_counts(c, g, tab, first_row, fronts_then=None):
                cols = slice(START[c], START[c] + WIDTH[c])
                region = a_chunk[c % 2][:, :, 0:WIDTH[c]].bitcast(FP32)
                sp.wait_ge(added["r" if tab is rtab2 else "a"][0], 16 * (1 + EDGE_COLS))
                if fronts_then is not None:
                    sp.wait_ge(front_done, fronts_then)
                sp.dma_start(region, tab[bass.ds(first_row, PADDED), cols].rearrange("(n p) d -> p n d", p=P)).then_inc(a_loaded[c % 2], 16)

            def load_row(u, ap, width):
                if u >= 2:
                    sp.wait_ge(*row_free(u - 2))
                sp.dma_start(rows[0:ap.shape[0], u % 2, 0:width], ap).then_inc(rows_loaded[u % 2], 16)

            def source(v):
                name, half, _, _ = SOURCES[v]
                for n in range(TILES):
                    load_row(ROW_AT["source", v, n], rows_of[name][P * n:P * n + ROWS[n], HALF * half:HALF * (half + 1)], HALF)

            def epoch_end(e):
                last, how, to, rest, _, _ = EPOCHS[e]
                v = next(v for v in range(len(SOURCES)) if FIRST_USE[v] == last + 1)
                for j in range(TILES + 4):
                    if how == "relu_add" and j < TILES:
                        load_row(ROW_AT["rest", e, j], rows_of[rest][P * j:P * j + ROWS[j], :], FEATURES)
                    n = j - 1
                    if 0 <= n < TILES:
                        if e in TAILS:
                            sp.wait_ge(tail_done, TILES * TAILS[e] + n + 1)
                        else:
                            sp.wait_ge(acc_done, GROUPS * last + 2 * (n + 1))
                        sp.dma_start(rows_of[to][P * n:P * n + ROWS[n], :], acc[0:ROWS[n], n, :]).then_inc(stored[n % 4], 16)
                    n = j - 4
                    if 0 <= n:
                        sp.wait_ge(stored[n % 4], 16 * (e * len(range(n % 4, TILES, 4)) + n // 4 + 1))
                        set_acc(e + 1, v, n)
                if e + 1 in ADDS:
                    load_bias(e + 1)

            def set_acc(e, v, n):
                sp.wait_ge(t_ready, TILES * v + n + 1)
                if e in ADDS:
                    start = rows_of[EPOCHS[e][3]][P * n:P * n + ROWS[n], :]
                else:
                    start = bias[EPOCHS[e][4]].rearrange("(o f) -> o f", o=1).to_broadcast((ROWS[n], FEATURES))
                sp.dma_start(acc[0:ROWS[n], n, :], start).then_inc(acc_set, 16)

            def load_bias(e):
                load_row(ROW_AT["bias", e, 0], bias[EPOCHS[e][4]].rearrange("(o f) -> o f", o=1).to_broadcast((P, FEATURES)), FEATURES)

            load_bias(0)
            s = 0
            while s < len(STEPS):
                graph, v, name, half = STEPS[s]
                g = G_BEFORE[s]
                if name == "rel":
                    with sp.Fori(0, RELATIONS) as r:
                        fronts_then = [sp.snap(FRONTS * (s + r) + o) for o in (2 * KT - FRONTS, 0, KT)]
                        first = sp.snap(r * PADDED)
                        load_weights(s + r, r * FEATURES + HALF * half, "rel")
                        for c, then in ((1, 0), (0, 1), (2, 2)):
                            load_counts(c, g + r, rtab2, first, fronts_then[then])
                    s += RELATIONS
                else:
                    if name != "edge":
                        load_weights(s, HALF * half, name)
                    if s == FIRST_GRAPH:
                        sp.wait_ge(hot_used, BATCHES)
                    if graph:
                        sp.wait_ge(front_done, FRONTS * s - FRONTS + 2 * KT)
                        load_counts(1, g, atab2, 0)
                        sp.wait_ge(front_done, FRONTS * s)
                        load_counts(0, g, atab2, 0)
                    if FIRST_USE[v] == s:
                        if s - 1 in EPOCH_END:
                            epoch_end(EPOCH_END[s - 1])
                        if not SOURCES[v][2]:
                            source(v)
                    if name == "edge":
                        load_edge_weights(s)
                    if graph:
                        sp.wait_ge(front_done, FRONTS * s + KT)
                        load_counts(2, g, atab2, 0)
                    s += 1
            e = len(EPOCHS) - 1
            for j in range(TILES + 1):
                if j < TILES:
                    load_row(ROW_AT["rest", e, j], rows_of["x3"][P * j:P * j + ROWS[j], :], FEATURES)
                    if j >= 2:
                        sp.wait_ge(out_ready, j - 1)
                    else:
                        sp.wait_ge(w_lo_ready, KT * len(STEPS))
                    sp.dma_start(w_raw[0:ROWS[j], j % 2, :], rows_of["u"][P * j:P * j + ROWS[j], :]).then_inc(u_loaded[j % 2], 16)
                n = j - 1
                if n >= 0:
                    sp.wait_ge(out_ready, n + 1)
                    sp.dma_start(out[P * n:P * n + ROWS[n], :], acc[0:ROWS[n], n, :]).then_inc(stored[n % 4], 16)
            for i in range(4):
                sp.wait_ge(stored[i], 16 * len(EPOCHS) * len(range(i, TILES, 4)))

        @block.gpsimd
        def _(pool):
            pool.memset(edges_i[:, :, :], 2000)
            pool.memset(edge_w[:, :], 0.0).then_inc(consts, 1)
            pool.memset(few_zeros[:, :], 0.0)
            pool.memset(zeros[:, :], 0.0).then_inc(consts, 1)
            pool.memset(ones_f[:, :], 1.0).then_inc(consts, 1)
            pool.memset(eps[:, :], EPS).then_inc(consts, 1)
            pool.iota(spare_i[:, :], pattern=[[P, 4]], base=0, channel_multiplier=1).then_inc(consts, 1)
            pool.iota(iota_i[:, :], pattern=[[1, P]], base=0, channel_multiplier=0).then_inc(consts, 1)
            pool.wait_ge(consts, 6)
            pool.affine_select(out=ident_f[:, :], in_=ones_f[:, :], compare_op=ALU.is_equal, fill=0.0, base=0,
                               pattern=[[-1, P]], channel_multiplier=1).then_inc(consts, 1)
            pool.affine_select(out=below[:, :], in_=ones_f[:, :], compare_op=ALU.is_gt, fill=0.0, base=0,
                               pattern=[[1, P]], channel_multiplier=-1).then_inc(consts, 1)
            for name, tabs in (("w", wtab), ("a", [atab]), ("r", [rtab])):
                for tab, link in zip(tabs, added[name]):
                    pool.dma_start(tab[tab.shape[0] - SPARE:].rearrange("(p c) o -> p (c o)", p=P), zeros[:, 0:4]).then_inc(link, 16)

            copied = 0
            for name, idx, val, tabs in (("w", idx_w, wsum, wtab), ("a", idx_a, cnt_a, [atab]),
                                                ("r", idx_r, cnt_r, [rtab])):
                sems, T = added[name], len(tabs)
                zeros_of = 16 * (ZERO_PIECES if name == "r" else T)
                with pool.Fori(0, QUADS // 2) as i:
                    for b in range(2):
                        q = 2 * i + b
                        over = pool.snap(pool.to_reg(16 * (1 + 4 * (i if T > 1 else q))))
                        copies = pool.snap(pool.to_reg(q + 1 + copied))
                        pool.wait_ge(idx_ready, q + 3)
                        pool.wait_ge(sems[b % T], over)
                        pool.tensor_copy(idx_slot[:, b, :], idx[:, bass.ds(4 * q, 4)])
                        pool.tensor_copy(val_slot[:, b, :], val[:, bass.ds(4 * q, 4)]).then_inc(slot_ready, 1)
                        pool.wait_ge(zeroed[name], zeros_of)
                        pool.wait_ge(slot_ready, copies)
                        for j in range(4):
                            pool.indirect_dma_start(
                                out=tabs[b % T], out_offset=bass.IndirectOffsetOnAxis(ap=idx_slot[:, b, j:j + 1], axis=0),
                                in_=val_slot[:, b, j:j + 1], in_offset=None, compute_op=ALU.add).then_inc(sems[b % T], 16)
                for j in range(T):
                    pool.wait_ge(sems[j], 16 * (1 + EDGE_COLS // T))
                copied += QUADS

        @block.scalar
        def _(act):
            def pt_slot_free(s, c):
                value = GROUPS * s + (0, -GROUPS + 2 * CHUNKS[1][1], 2 * CHUNKS[0][1])[c]
                if not isinstance(value, int) or value > 0:
                    act.wait_ge(dense_done, value)

            def split_weights_hi(s, k):
                if isinstance(s, int) and s < 2:
                    act.wait_ge(in_added, WSUM * s + (TABLES - 1) * (k + 1))
                else:
                    act.wait_ge(raw_loaded[k], 16 * (s + 1))
                if not (isinstance(s, int) and s == 0):
                    act.wait_ge(dense_done, GROUPS * s)
                nc.scalar.activation(w_hi[:, k, :], w_raw[:, k, :], ACT.Copy).then_inc(w_hi_ready, 1)

            def fronts(s, early_roots=None):
                for c in range(3):
                    if c == 2 and early_roots is not None:
                        for n in range(EARLY):
                            root_of_variance(early_roots, n)
                    for f in range(KT):
                        unit = KT * c + f
                        if f == 0:
                            pt_slot_free(s, c)
                        act.wait_ge(front_done, FRONTS * s + unit + 1)
                        nc.scalar.activation(pt_hi[c % 2][:, f, 0:WIDTH[c]], front_bank[unit % 3][:, 0:WIDTH[c]], ACT.Copy).then_inc(front_hi, 1)
                        if c == 0:
                            split_weights_hi(s, f)
                        if isinstance(s, int) and 0 <= FRONTS * (s - ZERO_FROM) + unit < ZERO_PIECES:
                            zero_piece(act, FRONTS * (s - ZERO_FROM) + unit)

            def root_of_variance(m, n):
                act.wait_ge(moments_ready, TILES * m + n + 1)
                nc.scalar.activation(std[0:ROWS[n], n:n + 1], moments[0:ROWS[n], n, 1:2], ACT.Sqrt, bias=eps[0:ROWS[n], :]).then_inc(std_ready, 1)

            def source_tile(v, n, m=None, e=None):
                name, half, from_acc, norm = SOURCES[v]
                r, count = ROWS[n], TILES * v + n + 1
                if from_acc:
                    s_in = acc[0:r, n, 0:HALF]
                    if e == 1:
                        act.wait_ge(tail_done, TILES * TAILS[1] + n + 1)
                    if e == 4:
                        act.wait_ge(acc_done, GROUPS * EPOCHS[4][0] + 2 * (n + 1))
                else:
                    u = ROW_AT["source", v, n]
                    s_in = rows[0:r, u % 2, 0:HALF]
                    act.wait_ge(rows_loaded[u % 2], 16 * (u // 2 + 1))
                if count > 2:
                    act.wait_ge(h_ready, count - 2)
                if m is not None:
                    act.wait_ge(norm_ready, TILES * m + n + 1)
                t = t_buf[0:r, n % 2, :]
                if norm:
                    nc.scalar.activation(t, s_in, ACT.Relu, scale=scale[0:r, n:n + 1], bias=shift[0:r, n:n + 1]).then_inc(t_ready, 1)
                else:
                    nc.scalar.activation(t, s_in, ACT.Copy).then_inc(t_ready, 1)
                if v and n == 0:
                    act.wait_ge(front_done, FRONTS * (LAST_USE[v - 1] + 1))
                act.wait_ge(t_ready, count)
                nc.scalar.activation(h_hi[0:r, n, :], t, ACT.Copy).then_inc(h_hi_ready, 1)

            def sources_after(s):
                v = STEPS[s + 1][1]
                if FIRST_USE[v] != s + 1:
                    return
                e = EPOCH_END.get(s)
                boundary(v, e, EARLY)

            def boundary(v, e, early=0):
                m = MOMENTS.get(e) if e is not None else None
                if m is not None:
                    for n in range(TILES):
                        if n >= early:
                            root_of_variance(m, n)
                        if n:
                            source_tile(v, n - 1, m, e)
                    source_tile(v, TILES - 1, m, e)
                else:
                    for n in range(TILES):
                        source_tile(v, n, None, e)

            def spread(q, b):
                if not isinstance(q, int) or q:
                    act.wait_ge(cast_done, q)
                act.wait_ge(keys_ready, 1)
                for j in range(4):
                    last = nc.scalar.activation(diag[:, b, j, :], ident_f[:, :], ACT.Copy, scale=key[:, bass.ds(4 * q + j, 1)])
                last.then_inc(diag_ready, 1)

            def copy_row(q, b):
                if not isinstance(q, int) or q:
                    act.wait_ge(same_ready, q + 1)
                act.wait_ge(cast_done, q + 2)
                nc.scalar.activation(key_row[:, b, :], cast_bank[b][:, :], ACT.Copy).then_inc(row_ready, 1)

            spread(0, 0)
            with act.Fori(0, QUADS // 2 - 1) as i:
                for b in range(2):
                    spread(2 * i + b + 1, 1 - b)
                    copy_row(2 * i + b, b)
            spread(QUADS - 1, 1)
            copy_row(QUADS - 2, 0)
            copy_row(QUADS - 1, 1)
            boundary(0, -1)
            s = 0
            while s < len(STEPS):
                if STEPS[s][2] == "rel":
                    with act.Fori(0, RELATIONS) as r:
                        fronts(s + r)
                    s += RELATIONS
                else:
                    fronts(s, MOMENTS.get(EPOCH_END.get(s)))
                    if s == FIRST_GRAPH - 1:
                        act.wait_ge(degrees_ready, 1)
                        nc.scalar.activation(deg_std[:, :], deg_std[:, :], ACT.Sqrt).then_inc(deg_root, 1)
                    s += 1
                if s < len(STEPS):
                    sources_after(s - 1)
            e = len(EPOCHS) - 1
            for n in range(TILES):
                r, u = ROWS[n], ROW_AT["rest", e, n]
                act.wait_ge(rows_loaded[u % 2], 16 * (u // 2 + 1))
                if n >= 2:
                    act.wait_ge(out_ready, n - 1)
                nc.scalar.activation(w_raw[0:r, 2 + n % 2, :], rows[0:r, u % 2, :], ACT.Relu, scale=scale[0:r, n:n + 1], bias=shift[0:r, n:n + 1])
                act.wait_ge(u_loaded[n % 2], 16 * (n // 2 + 1))
                nc.scalar.activation(w_raw[0:r, n % 2, :], w_raw[0:r, n % 2, :], ACT.Tanh).then_inc(gate_act, 1)

        @block.tensor
        def _(pe):
            def mm(o, l, r, start, stop, **kw):
                return nc.tensor.matmul(o, l, r, start=start, stop=stop, **kw)

            def cast(q, b):
                pe.wait_ge(diag_ready, q + 1)
                if not isinstance(q, int) or q:
                    pe.wait_ge(row_ready, q)
                mm(cast_bank[b][:, :], ones_f[:, :], diag[:, b, :, :].rearrange("p j c -> p (j c)"), True, True).then_inc(cast_done, 1)

            def sum_equal(q, b):
                pe.wait_ge(same_ready, q + 3)
                if not isinstance(q, int) or q:
                    pe.wait_ge(idx_ready, q + 1)
                for c in range(4):
                    sums = stat_bank[b][:, COLS * c:COLS * c + COLS]
                    for j in range(4):
                        last = mm(sums, same[:, b, j, P * c:P * c + P],
                                  values[:, bass.ds(COLS * (2 * (4 * q + j) + (1 if j < c else 0)), COLS)], j == 0, j == 3)
                        if j == 0:
                            mm(sums[:, 0:RELATIONS], before[:, b, c, :], values[:, bass.ds(COLS * (2 * (4 * q + c) + 1), RELATIONS)], False, False)
                last.then_inc(stat_done, 1)

            cast(0, 0)
            with pe.Fori(0, QUADS // 2 - 1) as i:
                for b in range(2):
                    cast(2 * i + b + 1, 1 - b)
                    sum_equal(2 * i + b, b)
            cast(QUADS - 1, 1)
            sum_equal(QUADS - 2, 0)
            sum_equal(QUADS - 1, 1)

            def count_batch(batch):
                pe.wait_ge(hot_ready, batch + 1)
                for j in range(BATCH):
                    ins = mm(deg_bank[:, 0:RELATIONS * TILES], hot_lo[:, batch % 2, j, :], hot_tile[:, batch % 2, j, :],
                             batch == 0 and j == 0, batch == BATCHES - 1 and j == BATCH - 1)
                ins.then_inc(hot_used, 1)

            def counts_loaded(c, g, with_self=False):
                if with_self:
                    pe.wait_ge(self_added, 3 * (g - FIRST_SELF) + c + 1)
                else:
                    pe.wait_ge(a_loaded[c % 2], 16 * (g + 1) if c == 1 else 16 * (2 * g + 1 + c // 2))

            def front(s, c, graph, v, g, with_self=False):
                a, b = CHUNKS[c]
                for f in range(KT):
                    unit = KT * c + f
                    cols = slice(P * f, P * f + P)
                    bank = front_bank[unit % 3]
                    if f == 0 and graph:
                        if c == 0:
                            pe.wait_ge(h_ready, TILES * (v + 1))
                        counts_loaded(c, g, with_self)
                    if not isinstance(s, int) or s or unit >= 3:
                        pe.wait_ge(front_lo, FRONTS * s + unit - 2)
                    if graph:
                        for n in range(TILES):
                            k = ROWS[n]
                            counts = a_chunk[c % 2][0:k, n, 0:WIDTH[c]]
                            mm(bank[:, 0:WIDTH[c]], h_hi[0:k, n, cols], counts, n == 0, False)
                            last = mm(bank[:, 0:WIDTH[c]], h_lo[0:k, n, cols], counts, False, n == TILES - 1)
                    else:
                        for n in range(a, b):
                            if f == 0:
                                pe.wait_ge(h_ready, TILES * v + n + 1)
                            k, first, second = ROWS[n], P * (n - a) // (2 * P) * 2 * P, (n - a) % 2
                            out, unit_of = bank[:, first:first + 2 * P], ident_wide[0:k, P * (1 - second):P * (3 - second)]
                            mm(out, h_hi[0:k, n, cols], unit_of, second == 0, False)
                            last = mm(out, h_lo[0:k, n, cols], unit_of, False, second == 1 or n == b - 1)
                    last.then_inc(front_done, 1)

            def dense(s, c):
                if c == 0:
                    pe.wait_ge(w_lo_ready, KT * (s + 1))
                pe.wait_ge(front_lo, FRONTS * s + KT * (c + 1))
                for n in range(*CHUNKS[c]):
                    m, o = ROWS[n], P * (n - CHUNKS[c][0])
                    for half in range(2):
                        group = 2 * n + half
                        if not isinstance(s, int) or s or group >= 4:
                            pe.wait_ge(acc_done, GROUPS * s + group - 3)
                        bank = dense_bank[group % 4][0:m, :]
                        cols = slice(512 * half, 512 * half + 512)
                        for f in range(KT):
                            hi, lo = pt_hi[c % 2][:, f, o:o + m], pt_lo[c % 2][:, f, o:o + m]
                            mm(bank, hi, w_hi[:, f, cols], f == 0, False)
                            mm(bank, hi, w_lo[:, f, cols], False, False)
                            last = mm(bank, lo, w_hi[:, f, cols], False, f == KT - 1)
                        last.then_inc(dense_done, 1)
                        if isinstance(s, int) and (s, group - 2) in BATCH_AT:
                            count_batch(BATCH_AT[s, group - 2])

            def step(s, graph, v, g, with_self=False):
                for c in range(2):
                    front(s, c, graph, v, g, with_self)
                dense(s, 0)
                front(s, 2, graph, v, g, with_self)
                dense(s, 1)
                dense(s, 2)

            s = 0
            while s < len(STEPS):
                graph, v, name, half = STEPS[s]
                g = G_BEFORE[s]
                if name == "rel":
                    with pe.Fori(0, RELATIONS) as r:
                        step(s + r, graph, v, g + r)
                    s += RELATIONS
                    continue
                step(s, graph, v, g, name == "gcn")
                s += 1

        @block.vector
        def _(dve):
            V = nc.vector
            count = [0]

            def link(ins):
                count[0] += 1
                ins.then_inc(small, 1)
                dve.wait_ge(small, count[0])

            dve.wait_ge(consts, 8)
            for i in (0, 2):
                V.tensor_scalar(ident_wide[:, P * i:P * i + P], ident_f[:, :], 0.0, None, ALU.mult)
            V.tensor_copy(ident[:, :], ident_f[:, :]).then_inc(row_ready, 1)
            V.memset(deg_inv[:, :], 1.0).then_inc(cast_done, 1)
            V.memset(deg_std[:, :], 1.0).then_inc(same_ready, 2)
            V.memset(rel_inv[:, :], 1.0).then_inc(stat_done, 1)
            V.memset(std[:, :], 1.0).then_inc(idx_ready, 2)
            link(V.tensor_copy(spare["w"][:, :], spare_i[:, :]))
            V.tensor_scalar(spare["a"][:, :], spare["w"][:, :], float(NA), None, ALU.add)
            link(V.tensor_scalar(spare["r"][:, :], spare["w"][:, :], float(RELATIONS * NA), None, ALU.add))
            dve.wait_ge(edges_in, 64)
            link(V.tensor_copy(edges_f[:, :, :], edges_i[:, :, :]))
            link(V.tensor_scalar(spare["w"][:, :], spare["w"][:, :], float(NW), None, ALU.add))
            src_f, dst_f, type_f = (edges_f[:, i, :] for i in range(3))
            V.scalar_tensor_tensor(out=key_w[:, :], in0=dst_f, scalar=float(FEATURES), in1=src_f, op0=ALU.mult, op1=ALU.add)
            V.scalar_tensor_tensor(out=key[:, :], in0=src_f, scalar=float(NODES), in1=dst_f, op0=ALU.mult, op1=ALU.add)
            V.scalar_tensor_tensor(out=src_row[:, :], in0=type_f, scalar=float(PADDED), in1=src_f, op0=ALU.mult, op1=ALU.add)
            V.tensor_scalar(valid[:, 0, :], src_f, float(FEATURES), None, ALU.is_lt)
            link(V.tensor_scalar(valid[:, 1, :], src_f, float(NODES), None, ALU.is_lt))
            V.scalar_tensor_tensor(out=key_r[:, :], in0=src_row[:, :], scalar=float(NODES), in1=dst_f, op0=ALU.mult, op1=ALU.add)
            link(V.scalar_tensor_tensor(out=valid[:, 0, :], in0=dst_f, scalar=float(FEATURES), in1=valid[:, 0, :], op0=ALU.is_lt, op1=ALU.mult))

            def quads(ap):
                return ap.rearrange("p (q j) -> p q j", j=4)

            rows_and_masks = (("w", key_w, 0), ("a", key, 1), ("r", key_r, 1))
            for name, k, ok in rows_and_masks:
                last = V.tensor_tensor(quads(off[name][:, :]), quads(k[:, :]), spare[name][:, :].unsqueeze(1).to_broadcast((P, QUADS, 4)), ALU.subtract)
            link(last)
            for name, k, ok in rows_and_masks:
                V.tensor_tensor(off[name][:, :], off[name][:, :], valid[:, ok, :], ALU.mult)
            link(V.tensor_copy(part[:, 0, :], edge_w[:, :]))
            link(V.tensor_tensor(edge_w[:, :], edge_w[:, :], part[:, 0, :], ALU.subtract))
            link(V.tensor_copy(part[:, 1, :], edge_w[:, :]))
            link(V.tensor_tensor(part[:, 2, :], edge_w[:, :], part[:, 1, :], ALU.subtract))
            by_edge = values[:, :].rearrange("p (t a c) -> p t a c", a=2, c=COLS)
            V.memset(by_edge[:, :, 0, 0:RELATIONS], 0.0)
            for t in range(RELATIONS):
                for a, c in ((0, RELATIONS + t), (1, t), (1, RELATIONS + t)):
                    V.tensor_scalar(by_edge[:, :, a, c:c + 1], type_f.unsqueeze(2), float(t), None, ALU.is_equal)
            for a in range(2):
                last = V.tensor_copy(by_edge[:, :, a, 2 * RELATIONS:COLS], part[:, :, :].rearrange("p c t -> p t c"))
            V.tensor_copy(iota[:, :], iota_i[:, :])
            V.tensor_scalar(lo_i[:, :], edges_i[:, 1, :], P - 1, None, ALU.bitwise_and).then_inc(small, 1)
            count[0] += 1
            dve.wait_ge(small, count[0])
            link(V.tensor_copy(dst_lo[:, :], lo_i[:, :]))
            link(V.tensor_tensor(dst_tile[:, :], dst_f, dst_lo[:, :], ALU.subtract))
            last = V.scalar_tensor_tensor(out=dst_tile[:, :], in0=dst_tile[:, :], scalar=float(RELATIONS) / P, in1=type_f, op0=ALU.mult, op1=ALU.add)
            last.then_inc(keys_ready, 1)
            dve.wait_ge(keys_ready, 1)

            def mark(q, b):
                dve.wait_ge(row_ready, q + 2)
                if not isinstance(q, int) or q:
                    dve.wait_ge(stat_done, q)
                for j in range(4):
                    last = V.tensor_scalar(same[:, b, j, :], key_row[:, b, :], key[:, bass.ds(4 * q + j, 1)], None, ALU.is_equal)
                last.then_inc(equal_done, 1)
                dve.wait_ge(equal_done, q + 1)
                for j in range(4):
                    last = V.tensor_tensor(before[:, b, j, :], same[:, b, j, P * j:P * j + P], below[:, :], ALU.mult)
                last.then_inc(same_ready, 1)

            def take_sums(q, b):
                cols = bass.ds(4 * q, 4)
                dve.wait_ge(stat_done, q + 2)
                sums = stat_bank[b][:, 0:4 * COLS].rearrange("p (j c) -> p j c", c=COLS)
                types = values[:, bass.ds(4 * q * 2 * COLS, 4 * 2 * COLS)].rearrange("p (j c) -> p j c", c=2 * COLS)[:, :, COLS:COLS + 2 * RELATIONS]
                V.tensor_tensor(by_type[:, b, :, :], sums[:, :, 0:2 * RELATIONS], types, ALU.mult).then_inc(sum_step, 1)
                V.tensor_reduce(tot[:, b, :, :], sums[:, :, 0:2 * RELATIONS].rearrange("p j (a c) -> p j a c", a=2), mybir.AxisListType.X, ALU.add)
                V.tensor_reduce(wsum[:, cols], sums[:, :, 2 * RELATIONS:COLS], mybir.AxisListType.X, ALU.add)
                dve.wait_ge(sum_step, 2 * q + 1)
                V.tensor_reduce(own[:, b, :, :], by_type[:, b, :, :].rearrange("p j (a c) -> p j a c", a=2), mybir.AxisListType.X, ALU.add).then_inc(sum_step, 1)
                dve.wait_ge(sum_step, 2 * q + 2)
                for m, (name, count_of) in enumerate((("w", tot), ("a", tot), ("r", own))):
                    last = V.scalar_tensor_tensor(out=idx_f[:, b, m, :], in0=count_of[:, b, :, 0], scalar=0.5, in1=off[name][:, cols],
                                                  op0=ALU.is_lt, op1=ALU.mult)
                last.then_inc(row_done, 1)
                V.tensor_copy(cnt_a[:, cols], tot[:, b, :, 1])
                V.tensor_copy(cnt_r[:, cols], own[:, b, :, 1])
                dve.wait_ge(row_done, q + 1)
                for m, (name, idx) in enumerate((("w", idx_w), ("a", idx_a), ("r", idx_r))):
                    last = V.tensor_tensor(idx[:, cols], idx_f[:, b, m, :], spare[name][:, :], ALU.add)
                last.then_inc(idx_ready, 1)

            def make_hot(batch):
                cols, b = slice(BATCH * batch, BATCH * batch + BATCH), batch % 2
                if batch > 1:
                    dve.wait_ge(hot_used, batch - 1)
                for out_t, of, width in ((hot_lo, dst_lo, P), (hot_tile, dst_tile, RELATIONS * TILES)):
                    last = V.tensor_tensor(out_t[:, b, :, :], iota[:, 0:width].unsqueeze(1).to_broadcast((P, BATCH, width)),
                                           of[:, cols].unsqueeze(2).to_broadcast((P, BATCH, width)), ALU.is_equal)
                last.then_inc(hot_ready, 1)

            def take_degrees():
                dve.wait_ge(hot_used, BATCHES)
                rel = deg_bank[:, 0:RELATIONS * TILES]
                link(V.tensor_reduce(deg_inv[:, :], rel.rearrange("p (n r) -> p n r", r=RELATIONS), mybir.AxisListType.X, ALU.add))
                V.tensor_scalar(rel_inv[:, :], rel, 1.0, None, ALU.max)
                V.tensor_scalar(deg_std[:, :], deg_inv[:, :], 1.0, None, ALU.add).then_inc(degrees_ready, 1)
                link(V.tensor_scalar(deg_inv[:, :], deg_inv[:, :], 1.0, None, ALU.max))
                V.reciprocal(deg_inv[:, :], deg_inv[:, :])
                V.reciprocal(rel_inv[:, :], rel_inv[:, :])

            def take_moments(m, n, e=-1):
                r = ROWS[n]
                if e >= 0 and e not in TAILS:
                    dve.wait_ge(acc_done, GROUPS * EPOCHS[e][0] + 2 * (n + 1))
                if TILES * m + n >= 2:
                    dve.wait_ge(moments_ready, TILES * m + n - 1)
                for i in range(2):
                    last = V.bn_stats(partial[0:r, n % 2, i, :], acc[0:r, n, HALF * i:HALF * (i + 1)])
                link(last)
                V.bn_aggr(moments[0:r, n, :], partial[0:r, n % 2, :, :].rearrange("p a b -> p (a b)")).then_inc(moments_ready, 1)

            def take_norm(m, n, e):
                r, c = ROWS[n], slice(n, n + 1)
                dve.wait_ge(std_ready, TILES * m + n + 1)
                link(V.reciprocal(scale[0:r, c], std[0:r, c]))
                if e == 2:
                    link(V.tensor_tensor(scale[0:r, c], scale[0:r, c], dinv[0:r, c], ALU.mult))
                V.scalar_tensor_tensor(out=shift[0:r, c], in0=moments[0:r, n, 0:1], scalar=-1.0, in1=scale[0:r, c],
                                       op0=ALU.mult, op1=ALU.mult).then_inc(norm_ready, 1)

            def source_lo(v, n):
                r = ROWS[n]
                dve.wait_ge(h_hi_ready, TILES * v + n + 1)
                V.tensor_tensor(h_lo[0:r, n, :], t_buf[0:r, n % 2, :], h_hi[0:r, n, :].bitcast(FP32), ALU.subtract).then_inc(h_ready, 1)

            def tail(e, n):
                last, how, _, _, _, _ = EPOCHS[e]
                r = ROWS[n]
                dve.wait_ge(acc_done, GROUPS * last + 2 * (n + 1))
                if how == "relu":
                    V.tensor_scalar(acc[0:r, n, :], acc[0:r, n, :], 0.0, None, ALU.max).then_inc(tail_done, 1)
                    return
                u = ROW_AT["rest", e, n]
                dve.wait_ge(rows_loaded[u % 2], 16 * (u // 2 + 1))
                rest = rows[0:r, u % 2, :]
                V.scalar_tensor_tensor(out=acc[0:r, n, :], in0=acc[0:r, n, :], scalar=0.0, in1=rest, op0=ALU.max, op1=ALU.add).then_inc(tail_done, 1)
                dve.wait_ge(tail_done, TILES * TAILS[e] + n + 1)

            def final(n):
                r, u = ROWS[n], ROW_AT["rest", len(EPOCHS) - 1, n]
                th, h3, x3, z = w_raw[0:r, n % 2, :], w_raw[0:r, 2 + n % 2, :], rows[0:r, u % 2, :], acc[0:r, n, :]
                dve.wait_ge(gate_act, n + 1)
                link(V.tensor_tensor(th, th, h3, ALU.subtract))
                dve.wait_ge(acc_done, GROUPS * LAST + 2 * (n + 1))
                V.tensor_tensor(h3, h3, x3, ALU.add)
                link(V.tensor_tensor(th, th, z, ALU.mult))
                V.tensor_tensor(z, th, h3, ALU.add).then_inc(out_ready, 1)

            def after_step(s):
                jobs = [[] for _ in range(GROUPS + 1)]
                if s == LAST:
                    for n in range(TILES):
                        jobs[max(9 + n, 2 * n + 2)].append(lambda n=n: final(n))
                    return jobs
                v = STEPS[s + 1][1]
                if FIRST_USE[v] != s + 1:
                    return jobs
                e = EPOCH_END.get(s)
                if e is None:
                    for n in range(TILES):
                        jobs[8 + n].append(lambda n=n: source_lo(v, n))
                    return jobs
                for n in range(TILES):
                    if e in TAILS:
                        jobs[2 * n + 2].append(lambda n=n: tail(e, n))
                    if EPOCHS[e][5]:
                        jobs[2 * n + 2].append(lambda n=n: take_moments(MOMENTS[e], n, e))
                        if n:
                            jobs[2 * n + 2].append(lambda n=n: take_norm(MOMENTS[e], n - 1, e))
                if EPOCHS[e][5]:
                    jobs[GROUPS].append(lambda: take_norm(MOMENTS[e], TILES - 1, e))
                for n in range(TILES):
                    jobs[min(GROUPS, max(9 + n, 2 * n + (6 if EPOCHS[e][5] else 4)))].append(lambda n=n: source_lo(v, n))
                return jobs

            def add_edge_weights(s):
                for k in range(KT):
                    for j in range(TABLES - 1):
                        q = WSUM * s + (TABLES - 1) * k + j
                        dve.wait_ge(in_loaded[q % WSUM], 16 * (q // WSUM + 1))
                        dve.wait_ge(raw_loaded[k], 16 * (s + 1))
                        if j:
                            dve.wait_ge(in_added, q)
                        V.tensor_tensor(w_raw[:, k, :], w_raw[:, k, :], in_buf[:, q % WSUM, :], ALU.add).then_inc(in_added, 1)

            def add_self_loops(g, c):
                a, b = CHUNKS[c]
                dve.wait_ge(a_loaded[c % 2], 16 * (g + 1) if c == 1 else 16 * (2 * g + 1 + c // 2))
                for n in range(a, b):
                    w = ROWS[n]
                    block_n = a_chunk[c % 2][0:w, n, P * (n - a):P * (n - a) + w]
                    last = V.tensor_tensor(block_n, block_n.bitcast(FP32), ident[0:w, 0:w].bitcast(FP32), ALU.add)
                last.then_inc(self_added, 1)

            def step(s, graph, name, half, r=None, jobs=None):
                def low_part(unit):
                    c, f = divmod(unit, KT)
                    dve.wait_ge(front_hi, FRONTS * s + unit + 1)
                    V.tensor_tensor(pt_lo[c % 2][:, f, 0:WIDTH[c]], front_bank[unit % 3][:, 0:WIDTH[c]],
                                    pt_hi[c % 2][:, f, 0:WIDTH[c]].bitcast(FP32), ALU.subtract).then_inc(front_lo, 1)

                def add_group(group):
                    n, o = divmod(group, 2)
                    m = ROWS[n]
                    dve.wait_ge(dense_done, GROUPS * s + group + 1)
                    tile = acc[0:m, n, 512 * o:512 * o + 512]
                    bank = dense_bank[group % 4][0:m, :]
                    if graph:
                        by = rel_inv[0:m, bass.ds(RELATIONS * n + r, 1)] if r is not None else (dinv if name == "gcn" else deg_inv)[0:m, n:n + 1]
                        V.scalar_tensor_tensor(out=tile, in0=bank, scalar=by, in1=tile, op0=ALU.mult, op1=ALU.add).then_inc(acc_done, 1)
                    else:
                        V.tensor_tensor(tile, bank, tile, ALU.add).then_inc(acc_done, 1)

                if name == "edge":
                    add_edge_weights(s)
                if name == "gcn":
                    add_self_loops(G_BEFORE[s], 0)
                    add_self_loops(G_BEFORE[s], 1)
                for f in range(KT):
                    low_part(f)
                    dve.wait_ge(w_hi_ready, KT * s + f + 1)
                    V.tensor_tensor(w_lo[:, f, :], w_raw[:, f, :], w_hi[:, f, :].bitcast(FP32), ALU.subtract).then_inc(w_lo_ready, 1)
                for f in range(KT):
                    low_part(KT + f)
                epoch = None
                if isinstance(s, int) and (s == 0 or s - 1 in EPOCH_END):
                    epoch = 0 if s == 0 else EPOCH_END[s - 1] + 1
                    if epoch:
                        dve.wait_ge(acc_set, 16 * TILES * epoch)
                    if epoch in ADDS:
                        u = ROW_AT["bias", epoch, 0]
                        dve.wait_ge(rows_loaded[u % 2], 16 * (u // 2 + 1))

                def after_group(group):
                    if isinstance(s, int) and (s, group) in BATCH_AT:
                        make_hot(BATCH_AT[s, group])
                    for job in (jobs[group] if jobs else ()):
                        job()

                def add_bias(n):
                    V.tensor_tensor(acc[0:ROWS[n], n, :], acc[0:ROWS[n], n, :], rows[0:ROWS[n], u % 2, :], ALU.add).then_inc(bias_added, 1)
                    dve.wait_ge(bias_added, TILES * ADDS[epoch] + n + 1)

                for group in range(2 * CHUNKS[0][1]):
                    if name == "gcn" and group == 6:
                        add_self_loops(G_BEFORE[s], 2)
                    if epoch in ADDS:
                        add_bias(group)
                    add_group(group)
                    after_group(group)
                if epoch in ADDS:
                    for n in range(2 * CHUNKS[0][1], TILES):
                        add_bias(n)
                for f in range(KT):
                    low_part(2 * KT + f)
                for group in range(2 * CHUNKS[0][1], GROUPS):
                    add_group(group)
                    after_group(group)
                after_group(GROUPS)

            mark(0, 0)
            with dve.Fori(0, QUADS // 2 - 1) as i:
                for b in range(2):
                    mark(2 * i + b + 1, 1 - b)
                    take_sums(2 * i + b, b)
            mark(QUADS - 1, 1)
            take_sums(QUADS - 2, 0)
            take_sums(QUADS - 1, 1)
            dve.wait_ge(x_in, 32)
            for n in range(TILES):
                take_moments(0, n)
                if n:
                    take_norm(0, n - 1, -1)
                if n > 1:
                    source_lo(0, n - 2)
            take_norm(0, TILES - 1, -1)
            source_lo(0, TILES - 2)
            source_lo(0, TILES - 1)
            s = 0
            while s < len(STEPS):
                graph, v, name, half = STEPS[s]
                if name == "rel":
                    with dve.Fori(0, RELATIONS - 1) as r:
                        step(s + r, graph, name, half, r)
                    s += RELATIONS
                    step(s - 1, graph, name, half, RELATIONS - 1, after_step(s - 1))
                    continue
                step(s, graph, name, half, None, after_step(s))
                if s == FIRST_GRAPH - 1:
                    take_degrees()
                if s == FIRST_GRAPH:
                    dve.wait_ge(deg_root, 1)
                    link(V.reciprocal(dinv[:, :], deg_std[:, :]))
                s += 1


_INPUTS = ["x", "src", "dst", "edge_type_8", "edge_weight", "L0_gnn_bias", "L1_gnn_W_self0", "L1_gnn_W_neigh0", "L1_gnn_b0",
           "L1_gnn_W_self1", "L1_gnn_W_neigh1", "L1_gnn_b1", "L2_gnn_W", "L2_gnn_b", "L3_gnn_weight", "L3_gnn_root",
           "L3_gnn_bias", "L3_gnn_w_gate", "L3_gnn_b_gate"]


def kernel(**inputs):
    import numpy as _np
    import concourse.bacc as _bacc
    from concourse import mybir as _mybir
    from concourse.bass_utils import run_bass_kernel_spmd as _run

    nc = _bacc.Bacc("TRN2", target_bir_lowering=False, num_devices=1)
    arrays, args = {}, []
    for name in _INPUTS:
        a = _np.ascontiguousarray(inputs[name])
        arrays[f"in_{name}"] = a
        args.append(nc.dram_tensor(f"in_{name}", a.shape, _mybir.dt.from_np(a.dtype), kind="ExternalInput").ap())
    out = nc.dram_tensor("out_0", (NODES, FEATURES), FP32, kind="ExternalOutput").ap()
    build(nc, *args, out)
    r = _run(nc, [arrays], core_ids=[0])
    return r.results[0]["out_0"]
```
